# Optimizing a Trainium2 kernel written in Bass

```python
import numpy as np
import jax
import jax.numpy as jnp

def _softmax(x, axis=-1):
    return jax.nn.softmax(x, axis=axis)

def _gelu(x):
    return jax.nn.gelu(x, approximate=True)

def _silu(x):
    return jax.nn.silu(x)

def _sigmoid(x):
    return jax.nn.sigmoid(x)

def _layernorm(x, axis=-1, eps=1e-05):
    m = jnp.mean(x, axis=axis, keepdims=True)
    v = jnp.var(x, axis=axis, keepdims=True)
    return (x - m) / jnp.sqrt(v + eps)

def _scatter_add(tgt, idx, src, axis=0):
    return tgt.at[idx].add(src)

def _segment_sum(src, seg, n):
    return jax.ops.segment_sum(src, seg, n)
kernel_name = 'mk_conv_preact_d4_conv_nhwc768_r4_9d506b'

def setup_inputs(seed: int=0):
    np.random.seed(seed)
    _w = jnp.asarray

    def _rec_inputs():
        import jax
        import jax.numpy as jnp
        _gk = jax.random.key(seed)
        x = -0.0005058 + 1 * jax.random.normal(jax.random.fold_in(_gk, 1), (2, 48, 48, 192), jnp.float32)
        return x
    x = _rec_inputs()

    def _L0_conv_setup():
        import jax, jax.numpy as jnp
        import numpy as np
        DIM = 192
        NUM_HEADS = 12
        HEAD_DIM = DIM // NUM_HEADS
        H = W = 48

        def _get_rel_pos(size, rel_pos):
            coords = jnp.arange(size)[:, None] - jnp.arange(size)[None, :] + (size - 1)
            return rel_pos[coords]
        key = jax.random.key(seed)
        ks = jax.random.split(key, 7)
        x = jax.random.normal(ks[0], (2, H, W, DIM), dtype=jnp.float32)
        qkv_w = jax.random.normal(ks[1], (DIM, 3 * DIM), dtype=jnp.float32) * DIM ** (-0.5)
        qkv_b = jax.random.normal(ks[2], (3 * DIM,), dtype=jnp.float32) * 0.02
        proj_w = jax.random.normal(ks[3], (DIM, DIM), dtype=jnp.float32) * DIM ** (-0.5)
        proj_b = jax.random.normal(ks[4], (DIM,), dtype=jnp.float32) * 0.02
        rel_pos_h = jax.random.normal(ks[5], (2 * H - 1, HEAD_DIM), dtype=jnp.float32) * 0.02
        rel_pos_w = jax.random.normal(ks[6], (2 * W - 1, HEAD_DIM), dtype=jnp.float32) * 0.02
        return {'x': x, 'qkv_w': qkv_w, 'qkv_b': qkv_b, 'proj_w': proj_w, 'proj_b': proj_b, 'rel_pos_h': rel_pos_h, 'rel_pos_w': rel_pos_w}
    _L0_conv_all = _L0_conv_setup()
    _L0_conv_in = {k: v for k, v in _L0_conv_all.items() if k in ('qkv_w', 'qkv_b', 'proj_w', 'proj_b', 'rel_pos_h', 'rel_pos_w')}
    del _L0_conv_all

    def _L1_conv_setup():
        import jax, jax.numpy as jnp
        import numpy as np
        B, H, W, C = (1, 16, 16, 192)
        NUM_HEADS = 12
        HEAD_DIM = C // NUM_HEADS
        key = jax.random.key(seed)
        ks = jax.random.split(key, 7)
        s = 0.02
        return {'imagelike_bhwc': jax.random.normal(ks[0], (B, H, W, C), dtype=jnp.float32), 'qkv_w': jax.random.normal(ks[1], (C, 3 * C), dtype=jnp.float32) * s, 'qkv_b': jax.random.normal(ks[2], (3 * C,), dtype=jnp.float32) * s, 'proj_w': jax.random.normal(ks[3], (C, C), dtype=jnp.float32) * s, 'proj_b': jax.random.normal(ks[4], (C,), dtype=jnp.float32) * s, 'rel_pos_h': jax.random.normal(ks[5], (2 * H - 1, HEAD_DIM), dtype=jnp.float32) * s, 'rel_pos_w': jax.random.normal(ks[6], (2 * W - 1, HEAD_DIM), dtype=jnp.float32) * s}
    _L1_conv_all = _L1_conv_setup()
    _L1_conv_in = {k: v for k, v in _L1_conv_all.items() if k in ('qkv_w', 'qkv_b', 'proj_w', 'proj_b', 'rel_pos_h', 'rel_pos_w')}
    del _L1_conv_all

    def _L2_conv_setup():
        import jax, jax.numpy as jnp
        import numpy as np
        NUM_HEADS = 12

        def _rel_pos_lookup(rel_pos, q_size, k_size):
            idx = jnp.arange(q_size)[:, None] - jnp.arange(k_size)[None, :] + (k_size - 1)
            return rel_pos[idx]
        key = jax.random.key(seed)
        ks = jax.random.split(key, 7)
        B, H, W, C = (8, 32, 32, 192)
        hd = C // NUM_HEADS
        s = 0.02
        return {'x': jax.random.normal(ks[0], (B, H, W, C), dtype=jnp.float32), 'qkv_w': jax.random.normal(ks[1], (C, 3 * C), dtype=jnp.float32) * s, 'qkv_b': jax.random.normal(ks[2], (3 * C,), dtype=jnp.float32) * s, 'proj_w': jax.random.normal(ks[3], (C, C), dtype=jnp.float32) * s, 'proj_b': jax.random.normal(ks[4], (C,), dtype=jnp.float32) * s, 'rel_pos_h': jax.random.normal(ks[5], (2 * H - 1, hd), dtype=jnp.float32) * s, 'rel_pos_w': jax.random.normal(ks[6], (2 * W - 1, hd), dtype=jnp.float32) * s}
    _L2_conv_all = _L2_conv_setup()
    _L2_conv_in = {k: v for k, v in _L2_conv_all.items() if k in ('qkv_w', 'qkv_b', 'proj_w', 'proj_b', 'rel_pos_h', 'rel_pos_w')}
    del _L2_conv_all

    def _L3_conv_setup():
        import jax, jax.numpy as jnp
        import numpy as np
        NUM_HEADS = 12

        def _get_rel_pos(size: int, rel_pos: jnp.ndarray) -> jnp.ndarray:
            coords = jnp.arange(size)[:, None] - jnp.arange(size)[None, :] + (size - 1)
            return rel_pos[coords]
        key = jax.random.key(seed)
        ks = jax.random.split(key, 6)
        C = 192
        hd = C // NUM_HEADS
        H = W = 32
        x = jax.random.normal(ks[0], (4, H, W, C), dtype=jnp.float32)
        Wqkv = jax.random.normal(ks[1], (C, 3 * C), dtype=jnp.float32) * 0.02
        Wproj = jax.random.normal(ks[2], (C, C), dtype=jnp.float32) * 0.02
        bproj = jax.random.normal(ks[3], (C,), dtype=jnp.float32) * 0.02
        rel_pos_h = jax.random.normal(ks[4], (2 * H - 1, hd), dtype=jnp.float32) * 0.02
        rel_pos_w = jax.random.normal(ks[5], (2 * W - 1, hd), dtype=jnp.float32) * 0.02
        return {'x': x, 'Wqkv': Wqkv, 'Wproj': Wproj, 'bproj': bproj, 'rel_pos_h': rel_pos_h, 'rel_pos_w': rel_pos_w}
    _L3_conv_all = _L3_conv_setup()
    _L3_conv_in = {k: v for k, v in _L3_conv_all.items() if k in ('Wqkv', 'Wproj', 'bproj', 'rel_pos_h', 'rel_pos_w')}
    del _L3_conv_all
    return {'x': x, 'L0_conv_qkv_w': _L0_conv_in['qkv_w'], 'L0_conv_qkv_b': _L0_conv_in['qkv_b'], 'L0_conv_proj_w': _L0_conv_in['proj_w'], 'L0_conv_proj_b': _L0_conv_in['proj_b'], 'L0_conv_rel_pos_h': _L0_conv_in['rel_pos_h'], 'L0_conv_rel_pos_w': _L0_conv_in['rel_pos_w'], 'L1_conv_qkv_w': _L1_conv_in['qkv_w'], 'L1_conv_qkv_b': _L1_conv_in['qkv_b'], 'L1_conv_proj_w': _L1_conv_in['proj_w'], 'L1_conv_proj_b': _L1_conv_in['proj_b'], 'L1_conv_rel_pos_h': _L1_conv_in['rel_pos_h'], 'L1_conv_rel_pos_w': _L1_conv_in['rel_pos_w'], 'L2_conv_qkv_w': _L2_conv_in['qkv_w'], 'L2_conv_qkv_b': _L2_conv_in['qkv_b'], 'L2_conv_proj_w': _L2_conv_in['proj_w'], 'L2_conv_proj_b': _L2_conv_in['proj_b'], 'L2_conv_rel_pos_h': _L2_conv_in['rel_pos_h'], 'L2_conv_rel_pos_w': _L2_conv_in['rel_pos_w'], 'L3_conv_Wqkv': _L3_conv_in['Wqkv'], 'L3_conv_Wproj': _L3_conv_in['Wproj'], 'L3_conv_bproj': _L3_conv_in['bproj'], 'L3_conv_rel_pos_h': _L3_conv_in['rel_pos_h'], 'L3_conv_rel_pos_w': _L3_conv_in['rel_pos_w']}

def reference(x, L0_conv_qkv_w, L0_conv_qkv_b, L0_conv_proj_w, L0_conv_proj_b, L0_conv_rel_pos_h, L0_conv_rel_pos_w, L1_conv_qkv_w, L1_conv_qkv_b, L1_conv_proj_w, L1_conv_proj_b, L1_conv_rel_pos_h, L1_conv_rel_pos_w, L2_conv_qkv_w, L2_conv_qkv_b, L2_conv_proj_w, L2_conv_proj_b, L2_conv_rel_pos_h, L2_conv_rel_pos_w, L3_conv_Wqkv, L3_conv_Wproj, L3_conv_bproj, L3_conv_rel_pos_h, L3_conv_rel_pos_w):
    import jax
    import jax.numpy as jnp

    def _L0_conv_ref(x, qkv_w, qkv_b, proj_w, proj_b, rel_pos_h, rel_pos_w):
        import jax, jax.numpy as jnp
        import numpy as np
        DIM = 192
        NUM_HEADS = 12
        HEAD_DIM = DIM // NUM_HEADS
        H = W = 48

        def _get_rel_pos(size, rel_pos):
            coords = jnp.arange(size)[:, None] - jnp.arange(size)[None, :] + (size - 1)
            return rel_pos[coords]
        B, h, w, dim = x.shape
        nh, hd = (NUM_HEADS, HEAD_DIM)
        S = h * w
        scale = hd ** (-0.5)
        qkv = (x.reshape(B, S, dim) @ qkv_w + qkv_b).reshape(B, S, 3, nh, hd)
        qkv = jnp.transpose(qkv, (2, 0, 3, 1, 4)).reshape(3, B * nh, S, hd)
        q, k, v = (qkv[0], qkv[1], qkv[2])
        attn = jnp.einsum('bqc,bkc->bqk', q * scale, k)
        Rh = _get_rel_pos(h, rel_pos_h)
        Rw = _get_rel_pos(w, rel_pos_w)
        r_q = q.reshape(B * nh, h, w, hd)
        rel_h = jnp.einsum('bhwc,hkc->bhwk', r_q, Rh)
        rel_w = jnp.einsum('bhwc,wkc->bhwk', r_q, Rw)
        attn = (attn.reshape(B * nh, h, w, h, w) + rel_h[:, :, :, :, None] + rel_w[:, :, :, None, :]).reshape(B * nh, S, S)
        attn = jax.nn.softmax(attn, axis=-1)
        out = (attn @ v).reshape(B, nh, h, w, hd)
        out = jnp.transpose(out, (0, 2, 3, 1, 4)).reshape(B, h, w, dim)
        return out @ proj_w + proj_b

    def _L1_conv_ref(imagelike_bhwc, qkv_w, qkv_b, proj_w, proj_b, rel_pos_h, rel_pos_w):
        import jax, jax.numpy as jnp
        import numpy as np
        B, H, W, C = (1, 16, 16, 192)
        NUM_HEADS = 12
        HEAD_DIM = C // NUM_HEADS
        b, h, w, c = imagelike_bhwc.shape
        n = h * w
        nh, hd = (NUM_HEADS, c // NUM_HEADS)
        scale = hd ** (-0.5)
        qkv = imagelike_bhwc @ qkv_w + qkv_b
        qkv = qkv.reshape(b, n, 3, nh, hd).transpose(2, 0, 3, 1, 4).reshape(3, b * nh, n, hd)
        q, k, v = (qkv[0], qkv[1], qkv[2])
        attn = jnp.einsum('bqd,bkd->bqk', q * scale, k)
        idx_h = jnp.arange(h)[:, None] - jnp.arange(h)[None, :] + (h - 1)
        idx_w = jnp.arange(w)[:, None] - jnp.arange(w)[None, :] + (w - 1)
        Rh = rel_pos_h[idx_h]
        Rw = rel_pos_w[idx_w]
        r_q = q.reshape(b * nh, h, w, hd)
        rel_h = jnp.einsum('bhwc,hkc->bhwk', r_q, Rh)
        rel_w = jnp.einsum('bhwc,wkc->bhwk', r_q, Rw)
        bias = (rel_h[:, :, :, :, None] + rel_w[:, :, :, None, :]).reshape(b * nh, n, n)
        attn = jax.nn.softmax(attn + bias, axis=-1)
        out = jnp.einsum('bqk,bkd->bqd', attn, v)
        out = out.reshape(b, nh, h, w, hd).transpose(0, 2, 3, 1, 4).reshape(b, h, w, c)
        return out @ proj_w + proj_b

    def _L2_conv_ref(x, qkv_w, qkv_b, proj_w, proj_b, rel_pos_h, rel_pos_w):
        import jax, jax.numpy as jnp
        import numpy as np
        NUM_HEADS = 12

        def _rel_pos_lookup(rel_pos, q_size, k_size):
            idx = jnp.arange(q_size)[:, None] - jnp.arange(k_size)[None, :] + (k_size - 1)
            return rel_pos[idx]
        B, H, W, C = x.shape
        nh = NUM_HEADS
        hd = C // nh
        scale = hd ** (-0.5)
        L = H * W
        qkv = x @ qkv_w + qkv_b
        qkv = qkv.reshape(B, L, 3, nh, hd).transpose(2, 0, 3, 1, 4).reshape(3, B * nh, L, hd)
        q, k, v = (qkv[0], qkv[1], qkv[2])
        attn = jnp.einsum('bqd,bkd->bqk', q * scale, k)
        Rh = _rel_pos_lookup(rel_pos_h, H, H)
        Rw = _rel_pos_lookup(rel_pos_w, W, W)
        r_q = q.reshape(B * nh, H, W, hd)
        rel_h = jnp.einsum('bhwc,hkc->bhwk', r_q, Rh)
        rel_w = jnp.einsum('bhwc,wkc->bhwk', r_q, Rw)
        attn = (attn.reshape(B * nh, H, W, H, W) + rel_h[:, :, :, :, None] + rel_w[:, :, :, None, :]).reshape(B * nh, L, L)
        attn = jax.nn.softmax(attn, axis=-1)
        out = jnp.einsum('bqk,bkd->bqd', attn, v)
        out = out.reshape(B, nh, H, W, hd).transpose(0, 2, 3, 1, 4).reshape(B, H, W, C)
        return out @ proj_w + proj_b

    def _L3_conv_ref(x, Wqkv, Wproj, bproj, rel_pos_h, rel_pos_w):
        import jax, jax.numpy as jnp
        import numpy as np
        NUM_HEADS = 12

        def _get_rel_pos(size: int, rel_pos: jnp.ndarray) -> jnp.ndarray:
            coords = jnp.arange(size)[:, None] - jnp.arange(size)[None, :] + (size - 1)
            return rel_pos[coords]
        B, H, W, C = x.shape
        hn = NUM_HEADS
        hd = C // hn
        scale = hd ** (-0.5)
        S = H * W
        qkv = x @ Wqkv
        qkv = qkv.reshape(B, S, 3, hn, hd)
        qkv = jnp.transpose(qkv, (2, 0, 3, 1, 4)).reshape(3, B * hn, S, hd)
        q, k, v = (qkv[0], qkv[1], qkv[2])
        Rh = _get_rel_pos(H, rel_pos_h)
        Rw = _get_rel_pos(W, rel_pos_w)
        r_q = q.reshape(B * hn, H, W, hd)
        rel_h = jnp.einsum('bhwc,hkc->bhwk', r_q, Rh)
        rel_w = jnp.einsum('bhwc,wkc->bhwk', r_q, Rw)
        bias = rel_h[..., :, None] + rel_w[..., None, :]
        bias = bias.reshape(B * hn, S, S)
        scores = scale * jnp.einsum('bqc,bkc->bqk', q, k) + bias
        attn = jax.nn.softmax(scores, axis=-1)
        out = jnp.einsum('bqk,bkc->bqc', attn, v)
        out = out.reshape(B, hn, H, W, hd)
        out = jnp.transpose(out, (0, 2, 3, 1, 4)).reshape(B, H, W, C)
        return out @ Wproj + bproj

    def _gn(v, G=32, eps=1e-05):
        B_, H_, W_, C_ = v.shape
        g = v.reshape(B_, H_, W_, G, C_ // G)
        m = jnp.mean(g, axis=(1, 2, 4), keepdims=True)
        s = jnp.var(g, axis=(1, 2, 4), keepdims=True)
        return ((g - m) / jnp.sqrt(s + eps)).reshape(v.shape)

    def _ln_c(v, eps=1e-06):
        m = jnp.mean(v, axis=-1, keepdims=True)
        s = jnp.var(v, axis=-1, keepdims=True)
        return (v - m) / jnp.sqrt(s + eps)

    def _ln_t(v, eps=1e-05):
        m = jnp.mean(v, axis=-1, keepdims=True)
        s = jnp.var(v, axis=-1, keepdims=True)
        return (v - m) / jnp.sqrt(s + eps)

    def _to_tokens(v):
        B_, H_, W_, C_ = v.shape
        return v.reshape(B_, H_ * W_, C_)

    def _from_tokens(t, like):
        return t.reshape(like.shape)
    x = x + _L0_conv_ref(_gn(x), L0_conv_qkv_w, L0_conv_qkv_b, L0_conv_proj_w, L0_conv_proj_b, L0_conv_rel_pos_h, L0_conv_rel_pos_w)
    x = x + _L1_conv_ref(_gn(x), L1_conv_qkv_w, L1_conv_qkv_b, L1_conv_proj_w, L1_conv_proj_b, L1_conv_rel_pos_h, L1_conv_rel_pos_w)
    x = x + _L2_conv_ref(_gn(x), L2_conv_qkv_w, L2_conv_qkv_b, L2_conv_proj_w, L2_conv_proj_b, L2_conv_rel_pos_h, L2_conv_rel_pos_w)
    x = x + _L3_conv_ref(_gn(x), L3_conv_Wqkv, L3_conv_Wproj, L3_conv_bproj, L3_conv_rel_pos_h, L3_conv_rel_pos_w)
    return x

_drawn_inputs = setup_inputs


def setup_inputs(seed=0):
    import zlib

    import numpy as np

    out = dict(_drawn_inputs(seed))
    spreads = {}
    factors = {'L0_conv_proj_b': 2.916,
     'L0_conv_rel_pos_h': 8.0,
     'L0_conv_rel_pos_w': 8.0,
     'L1_conv_qkv_w': 8.0,
     'L1_conv_qkv_b': 8.0,
     'L1_conv_proj_w': 8.0,
     'L1_conv_proj_b': 2.938,
     'L1_conv_rel_pos_h': 8.0,
     'L1_conv_rel_pos_w': 8.0,
     'L2_conv_qkv_w': 8.0,
     'L2_conv_qkv_b': 8.0,
     'L2_conv_proj_w': 8.0,
     'L2_conv_proj_b': 9.023,
     'L2_conv_rel_pos_h': 8.0,
     'L2_conv_rel_pos_w': 8.0,
     'L3_conv_Wqkv': 8.0,
     'L3_conv_Wproj': 8.0,
     'L3_conv_bproj': 18.961,
     'L3_conv_rel_pos_h': 8.0,
     'L3_conv_rel_pos_w': 8.0}
    for name, (base, spread) in spreads.items():
        noise = np.random.default_rng([zlib.crc32(name.encode()), seed]).standard_normal(out[name].shape)
        drawn = base * np.exp(spread * noise) if base else spread * noise
        out[name] = jnp.asarray(drawn.astype(out[name].dtype))
    for name, factor in factors.items():
        out[name] = (out[name] * factor).astype(out[name].dtype)
    return out
```

```python
from contextlib import ExitStack

import concourse.bass as bass
from concourse import mybir

F32 = mybir.dt.float32
F32R = mybir.dt.float32r
ACT = mybir.ActivationFunctionType
ALU = mybir.AluOpType
AX = mybir.AxisListType

LAYERS, IMAGES, SIDE, CH, HEADS = 4, 2, 48, 192, 12
GROUPS, EPS = 32, 1e-5
DH = CH // HEADS
N = SIDE * SIDE
TOK = IMAGES * N
HALF = CH // 2
UNITS = IMAGES * HEADS
P = 128
KT = N // P
BLK = 384
GRP = N // BLK
QG = BLK // P
SBW = 2 * BLK
SB = N // BLK
SCB = 3
AXB = 3
NSB = KT * SB
SLOTS = 4
QUART = N // 4
OH = QUART // 2
NRM = 2 * OH // AXB
TBW = 224
RELW = 112
MAXB = 5
REL = 2 * GRP
MAXF = KT * MAXB
PF = N // SBW
QKF = IMAGES * 3 * PF
VF = TOK // P // 4
PJF = 2 * TOK // SBW
SPLIT_AT = 60
ATTEND_AT = [2, 5]
GN_LINKS = 14


def schedule():
    at = [[("relw", r)] for r in range(GRP)] + [[("relh", r)] for r in range(GRP)]
    at += [[("norm", f)] for f in range(AXB)] + [[]]
    rest = []
    for g in range(GRP):
        for k in range(QG * MAXB):
            rest.append(("max", g * QG * MAXB + k))
            if g and k == 3:
                rest.append(("bias", g - 1))
    rest.append(("bias", GRP - 1))
    places = NSB - len(at)
    cuts = [-(-len(rest) * k // places) for k in range(places + 1)]
    return at + [rest[cuts[k]:cuts[k + 1]] for k in range(places)]


def build(nc, a):
    plan = schedule()
    with ExitStack() as ctx:
        def sb(name, shape, dt=F32):
            return ctx.enter_context(nc.sbuf_tensor(name, shape, dt))

        def ps(name, shape):
            return ctx.enter_context(nc.psum_tensor(name, shape, F32))

        def sem(name):
            return ctx.enter_context(nc.semaphore(name))

        qk_dram = nc.dram_tensor("qk_scratch", (2 * CH, TOK), F32).ap()
        ao_dram = nc.dram_tensor("attention_scratch", (CH, TOK), F32).ap()

        x = sb("x", [HALF, 2, TOK])
        region = sb("region", [P, SLOTS * N])
        xn = region[0:HALF, :].rearrange("p (t n) -> p t n", t=2)
        probs = region[:, :].rearrange("p (s n) -> p s n", s=SLOTS)
        vall = sb("vall", [P, TOK // P, CH])
        vu = sb("vu", [P, 2, KT, 32])
        full = sb("full", [P, N])
        qkrep = sb("qkrep", [P, N])
        qkhl = sb("qkhl", [P, N], F32R)
        hi = sb("hi", [P, 2, N], F32R)
        lo = sb("lo", [P, 2, N], F32R)
        keys = sb("keys", [P, 2, N], F32R)
        wqkv = sb("wqkv", [HALF, 2, 3 * CH])
        wproj = sb("wproj", [HALF, 2, CH])
        tabf = sb("tabf", [P, 2, TBW])
        tab = sb("tab", [P, 2, TBW], F32R)
        ident = sb("ident", [P, P])
        rowsel = sb("rowsel", [P, P], F32R)
        densel = sb("densel", [P, P])
        gmat = sb("gmat", [HALF, HALF])
        hlmask = sb("hlmask", [P, 2])
        qkscale = sb("qkscale", [P, 3])
        bqk = sb("bqk", [P, 3])
        bqks = sb("bqks", [P, 3])
        bv = sb("bv", [1, CH])
        ones = sb("ones", [1, P])
        bproj = sb("bproj", [HALF, 2])
        mpart = sb("mpart", [P, 2, QG, MAXB])
        mcol = sb("mcol", [P, 2, QG])
        diag = sb("diag", [P, 2, QG, P], F32R)
        oraw = sb("oraw", [P, 2, OH])
        orec = sb("orec", [P, 2, OH])
        onorm = sb("onorm", [P, 2, OH])
        tabh = orec[:, :, 0:TBW]
        stats = onorm[0:HALF, 0, 0:4 * GRP * 6].rearrange("p (i s k) -> p i s k", i=4, k=6)
        mv = sb("mv", [HALF, 4, 2])
        gm = sb("gm", [HALF, 4])
        gt = sb("gt", [HALF, 4])
        gv = sb("gv", [HALF, 4])
        gs = sb("gs", [HALF, 4])
        gr = sb("gr", [HALF, 4])
        gn = sb("gn", [HALF, 4])

        work = ps("work", [P, SCB + AXB, 512])
        score = work[:, 0:SCB, :]
        aux = work[:, SCB:SCB + AXB, :]
        proj = work[:, 0:4, :].rearrange("p (f a) q -> p f a q", a=2)
        out_ps = ps("out_ps", [P, 2, 512])

        const_in = sem("const_in")
        weights_in = sem("weights_in")
        const_set = sem("const_set")
        pool_set = sem("pool_set")
        gn_link = sem("gn_link")
        gn_sum = sem("gn_sum")
        gn_ready = sem("gn_ready")
        gn_root = sem("gn_root")
        xn_ready = sem("xn_ready")
        qk_filled = sem("qk_filled")
        qk_read = sem("qk_read")
        qk_stored = [sem("qk_stored_full"), sem("qk_stored_rep")]
        rep_in = sem("rep_in")
        full_in = sem("full_in")
        split_high = sem("split_high")
        split = sem("split")
        key_in = sem("key_in")
        vu_ready = sem("vu_ready")
        rel_filled = sem("rel_filled")
        rel_read = sem("rel_read")
        first_hi = sem("first_hi")
        max_filled = sem("max_filled")
        max_read = sem("max_read")
        mx_link = sem("mx_link")
        diag_ready = sem("diag_ready")
        bias_filled = sem("bias_filled")
        bias_read = sem("bias_read")
        hi_ready = sem("hi_ready")
        lo_ready = sem("lo_ready")
        score_filled = sem("score_filled")
        score_read = sem("score_read")
        slot_free = sem("slot_free")
        o_read = sem("o_read")
        norm_filled = sem("norm_filled")
        norm_read = sem("norm_read")
        o_ready = sem("o_ready")
        o_stored = sem("o_stored")
        o_loaded = sem("o_loaded")
        pj_filled = sem("pj_filled")
        pj_read = sem("pj_read")
        stored = sem("stored")

        def run_units(eng, layer, first, phase, last):
            base = layer * UNITS
            first(eng.snap(base), layer)
            phase(eng.snap(base), 0, 0, False, True, True)
            with eng.Fori(0, HEADS - 2) as h:
                phase(eng.snap(base + h * 2 + 1), h, 1, True, True, True)
                phase(eng.snap(base + h * 2 + 2), h + 1, 0, True, True, True)
            phase(eng.snap(base + UNITS - 3), HEADS - 2, 1, True, True, True)
            phase(eng.snap(base + UNITS - 2), HEADS - 1, 0, True, True, False)
            phase(eng.snap(base + UNITS - 1), HEADS - 1, 1, True, False, False)
            last(eng.snap(base + UNITS))

        block = ctx.enter_context(nc.Block())

        @block.sync
        def _(sp):
            sp.dma_start(full[:, :], a["key_onehot"]).then_inc(const_in, 16)
            for dst, name in ((ident[:, :], "ident"), (qkrep[:, 0:P], "rowsel"), (densel[:, :], "densel"),
                              (gmat[:, :], "gmat"), (hlmask[:, :], "hlmask"), (qkscale[:, :], "qkscale")):
                sp.dma_start(dst, a[name]).then_inc(const_in, 16)
            for t in range(2):
                sp.dma_start(x[:, t, :], a["x"][t * HALF:(t + 1) * HALF, :]).then_inc(const_in, 16)
            def rep_load(h, b):
                for s in range(2):
                    for k in range(2):
                        for r in range(2):
                            p = s * 64 + k * 32 + r * DH
                            sp.dma_start(qkrep[p:p + DH, :],
                                         qk_dram[bass.ds(h * DH + k * CH, DH), b * N:(b + 1) * N]).then_inc(rep_in, 16)

            def full_load(h, b):
                for p in (48, 112):
                    sp.dma_start(full[p:p + DH, :],
                                 qk_dram[bass.ds(h * DH, DH), b * N:(b + 1) * N]).then_inc(full_in, 16)

            def key_load(b):
                for p, src in ((48, 32), (112, 96)):
                    sp.dma_start(keys[p:p + DH, b, :].bitcast(F32), qkhl[src:src + DH, :].bitcast(F32)).then_inc(key_in, 16)

            def first(u, layer):
                for stored_from in qk_stored:
                    sp.wait_ge(stored_from, (layer + 1) * 3 * 16)
                rep_load(0, 0)
                full_load(0, 0)
                sp.wait_ge(split, u + 1)
                key_load(0)
                rep_load(0, 1)

            def out_store(u, h, b):
                sp.wait_ge(o_ready, u)
                sp.wait_ge(const_set, 5)
                for j in range(4):
                    sp.dma_start(ao_dram[bass.ds(h * DH, DH), b * N + j * QUART:b * N + (j + 1) * QUART],
                                 onorm[32 * j:32 * j + DH, :, :].rearrange("p a c -> p (a c)")).then_inc(o_stored, 16)

            def phase(u, h, b, prev, nxt, nxt2):
                if nxt:
                    sp.wait_ge(lo_ready, (u + 1) * GRP)
                    full_load(h + b, 1 - b)
                    sp.wait_ge(split, u + 2)
                    key_load(1 - b)
                if nxt2:
                    rep_load(h + 1, b)
                if prev:
                    out_store(u, h - 1 + b, 1 - b)

            def last(u):
                out_store(u, HEADS - 1, 1)

            with sp.Fori(0, LAYERS) as layer:
                def weight(dst, name):
                    letters = " ".join("abcd"[:len(a[name].shape) - 2])
                    src = a[name][bass.ds(layer, 1)].rearrange(f"o p {letters} -> (o p) {letters}")
                    sp.dma_start(dst, src).then_inc(weights_in, 16)

                sp.wait_ge(pj_read, layer * PJF)
                sp.wait_ge(const_set, 5)
                weight(wqkv[:, 0, :], "wqkv0")
                weight(wqkv[:, 1, :], "wqkv1")
                weight(wproj[:, 0, :], "wproj0")
                weight(wproj[:, 1, :], "wproj1")
                weight(bqk[:, :], "bqk")
                weight(bv[:, :], "bv")
                weight(bproj[:, :], "bproj")
                for p in (0, 16, 64, 80):
                    weight(tabf[p:p + DH, :, :], "rel")
                for k in range(IMAGES * 3):
                    b, m = divmod(k, 3)
                    sp.wait_ge(qk_read, layer * (QKF + VF) + PF * (k + 1))
                    sp.dma_start(qk_dram[m * P:(m + 1) * P, b * N:(b + 1) * N],
                                 (full, qkrep)[k % 2][:, :]).then_inc(qk_stored[k % 2], 16)
                run_units(sp, layer, first, phase, last)
                sp.wait_ge(o_stored, (layer + 1) * UNITS * 64)
                for t in range(2):
                    sp.dma_start(xn[:, t, :], ao_dram[t * HALF:(t + 1) * HALF, :]).then_inc(o_loaded, 16)
            sp.wait_ge(pj_read, LAYERS * PJF)
            for t in range(2):
                sp.dma_start(a["out"][t * HALF:(t + 1) * HALF, :], x[:, t, :]).then_inc(stored, 16)
            sp.wait_ge(stored, 32)

        @block.gpsimd
        def _(pool):
            pool.memset(vu[:, :, :, DH:32], 0.0).then_inc(pool_set, 1)
            pool.wait_ge(pool_set, 1)
            pool.memset(vu[:, :, :, DH:DH + 1], 1.0).then_inc(pool_set, 1)
            pool.wait_ge(pool_set, 2)

            def split_low(j):
                pool.wait_ge(split_high, j + 1)
                pool.tensor_tensor(qkhl[64:128, :], qkrep[64:128, :], qkhl[64:128, :].bitcast(F32),
                                   ALU.subtract).then_inc(split, 1)

            def values(b, h):
                pool.tensor_copy(vu[:, b, :, 0:DH],
                                 vall[:, b * KT:(b + 1) * KT, bass.ds(h * DH, DH)]).then_inc(vu_ready, 1)

            def prepare(j, h, b, split_next):
                for g in range(GRP):
                    cols = slice(g * BLK, (g + 1) * BLK)
                    if g == 0:
                        pool.wait_ge(split, j + 1)
                    if g == 4 and split_next:
                        pool.wait_ge(split, j + 2)
                    pool.wait_ge(hi_ready, j * GRP + g + 1)
                    pool.tensor_tensor(lo[:, b, cols], full[:, cols], hi[:, b, cols].bitcast(F32),
                                       ALU.subtract).then_inc(lo_ready, 1)
                    if g == 0:
                        values(b, h)
                    if g == 3 and split_next:
                        pool.wait_ge(lo_ready, j * GRP + 4)
                        split_low(j + 1)

            def first(u, layer):
                pool.wait_ge(qk_read, (layer + 1) * (QKF + VF))
                split_low(u)
                prepare(u, 0, 0, False)
                pool.wait_ge(lo_ready, (u + 1) * GRP)
                split_low(u + 1)

            def normalise(u):
                pool.wait_ge(norm_read, AXB * u)
                pool.wait_ge(o_stored, 64 * (u - 1))
                pool.tensor_tensor(onorm[:, :, :], oraw[:, :, :], orec[:, :, :], ALU.mult).then_inc(o_ready, 1)

            def phase(u, h, b, prev, nxt, nxt2):
                if prev:
                    pool.wait_ge(slot_free, u * KT + SLOTS)
                    normalise(u)
                if nxt:
                    prepare(u + 1, h + b, 1 - b, nxt2)

            with pool.Fori(0, LAYERS) as layer:
                run_units(pool, layer, first, phase, normalise)

        @block.scalar
        def _(act):
            def rel_out(j, kind, r, n):
                act.wait_ge(rel_filled, j * REL + n + 1)
                bank = aux[:, n % AXB, 0:BLK]
                if kind == "relh":
                    act.activation(full[0:SIDE, r * BLK:(r + 1) * BLK], bank[0:SIDE, :], ACT.Copy)\
                       .then_inc(rel_read, 1)
                else:
                    to = full[64:64 + SIDE, :].rearrange("p (h w) -> p h w", w=SIDE)[:, :, 8 * r:8 * r + 8]
                    act.activation(to, bank[64:64 + SIDE, :].rearrange("p (w h) -> p h w", w=8), ACT.Copy)\
                       .then_inc(rel_read, 1)

            def high(j, b, g, ready):
                cols = slice(g * BLK, (g + 1) * BLK)
                act.activation(hi[:, b, cols], full[:, cols], ACT.Copy).then_inc(ready, 1)

            def high_behind(j, b, kind, f):
                if kind == "relh":
                    act.wait_ge(rel_read, j * REL + GRP + f + 1)
                    if f == 0:
                        act.wait_ge(full_in, 32 * (j + 1))
                    high(j, b, f, first_hi)
                elif kind == "bias":
                    act.wait_ge(bias_read, j * GRP + f + 1)
                    high(j, b, f, hi_ready)

            def split_qk(j):
                act.wait_ge(rep_in, 128 * (j + 1))
                act.activation(qkhl[:, :], qkrep[:, :], ACT.Copy).then_inc(split_high, 1)

            rels = [f for fills in plan for f in fills if f[0] in ("relw", "relh")]

            def first(u, layer):
                split_qk(u)
                for n, (kind, r) in enumerate(rels):
                    rel_out(u, kind, r, n)
                    high_behind(u, 0, kind, r)
                for g in range(GRP):
                    high_behind(u, 0, "bias", g)
                act.wait_ge(key_in, 32 * (u + 1))
                split_qk(u + 1)

            def phase(u, h, b, prev, nxt, nxt2):
                n, late = 0, []
                for k in range(NSB):
                    c, s = divmod(k, SB)
                    if s == 0:
                        act.wait_ge(slot_free, u * KT + c + 1)
                    act.wait_ge(score_filled, u * NSB + k + 1)
                    act.activation(probs[:, (KT * b + c) % SLOTS, s * BLK:(s + 1) * BLK],
                                   score[:, k % SCB, 0:BLK], ACT.Exp).then_inc(score_read, 1)
                    if not nxt:
                        continue
                    for f in late:
                        high_behind(u + 1, 1 - b, "bias", f)
                    late = [f for kind, f in plan[k] if kind == "bias"]
                    for kind, r in plan[k]:
                        if kind in ("relw", "relh"):
                            if n == 0:
                                act.wait_ge(lo_ready, (u + 1) * GRP)
                            rel_out(u + 1, kind, r, n)
                            high_behind(u + 1, 1 - b, kind, r)
                            n += 1
                    if k == SPLIT_AT and nxt2:
                        act.wait_ge(key_in, 32 * (u + 2))
                        split_qk(u + 2)
                if nxt:
                    for f in late:
                        high_behind(u + 1, 1 - b, "bias", f)

            with act.Fori(0, LAYERS) as layer:
                act.wait_ge(gn_ready, layer * 3 + 3)
                act.activation(gs[:, :], gv[:, :], ACT.Sqrt).then_inc(gn_root, 1)
                for f in range(QKF):
                    k, s = divmod(f, PF)
                    if s == 0 and k >= 2:
                        act.wait_ge(qk_stored[k % 2], (layer * 3 + k // 2) * 16)
                    act.wait_ge(qk_filled, layer * (QKF + VF) + f + 1)
                    m = k % 3
                    to = (full, qkrep)[k % 2][:, s * SBW:(s + 1) * SBW].rearrange("p (a q) -> p a q", a=2)
                    act.activation(to, proj[:, f % 2, :, 0:BLK], ACT.Identity, bias=bqks[:, m:m + 1],
                                   scale=qkscale[:, m:m + 1]).then_inc(qk_read, 1)
                for v in range(VF):
                    f = QKF + v
                    act.wait_ge(qk_filled, layer * (QKF + VF) + f + 1)
                    act.activation(vall[:, 4 * v:4 * v + 4, :].rearrange("p (a t) c -> p a (t c)", a=2),
                                   proj[:, f % 2, :, 0:BLK], ACT.Copy).then_inc(qk_read, 1)
                run_units(act, layer, first, phase, lambda u: None)

        @block.vector
        def _(dve):
            dve.memset(tabf[:, :, :], 0.0).then_inc(const_set, 1)
            dve.memset(ones[:, :], 1.0).then_inc(const_set, 1)
            dve.wait_ge(const_in, 16 * 9)
            dve.tensor_copy(keys[:, 0, :], full[:, :]).then_inc(const_set, 1)
            dve.tensor_copy(keys[:, 1, :], full[:, :]).then_inc(const_set, 1)
            dve.tensor_copy(rowsel[:, :], qkrep[:, 0:P]).then_inc(const_set, 1)
            dve.wait_ge(const_set, 5)

            def key_max(j, f, bank):
                t, m = divmod(f, MAXB)
                g = t // QG
                w = min(512, N - 512 * m)
                dve.wait_ge(max_filled, j * MAXF + f + 1)
                dve.tensor_reduce(mpart[:, g % 2, t % QG, m:m + 1], aux[:, bank, 0:w], AX.X, ALU.max)\
                   .then_inc(max_read, 1)
                if f % (QG * MAXB) == QG * MAXB - 1:
                    dve.wait_ge(max_read, j * MAXF + f + 1)
                    dve.tensor_reduce(mcol[:, g % 2, :], mpart[:, g % 2, :, :], AX.X, ALU.max).then_inc(mx_link, 1)
                    dve.wait_ge(mx_link, j * GRP + g + 1)
                    for t in range(QG):
                        last = dve.tensor_scalar(diag[:, g % 2, t, :], ident[:, :], mcol[:, g % 2, t:t + 1], None,
                                                 ALU.mult)
                    last.then_inc(diag_ready, 1)

            def subtract_max(j, g, bank):
                cols = slice(g * BLK, (g + 1) * BLK)
                dve.wait_ge(bias_filled, j * GRP + g + 1)
                dve.tensor_tensor(full[:, cols], full[:, cols], aux[:, bank, 0:BLK], ALU.subtract)\
                   .then_inc(bias_read, 1)

            def sums_out(u):
                dve.wait_ge(slot_free, u * KT + SLOTS)
                dve.wait_ge(o_ready, u - 1)
                dve.tensor_copy(oraw[:, :, :], out_ps[:, :, 0:OH]).then_inc(o_read, 1)

            def reciprocal(u, f):
                dve.wait_ge(norm_filled, AXB * (u - 1) + f + 1)
                dve.reciprocal(orec[:, :, :].rearrange("p a q -> p (a q)")[:, f * NRM:(f + 1) * NRM],
                               aux[:, f, 0:NRM]).then_inc(norm_read, 1)

            def fills(u, prev, nxt):
                n = 0
                for items in plan:
                    for kind, f in items:
                        if kind == "norm":
                            if prev:
                                reciprocal(u, f)
                            continue
                        if nxt and kind == "max":
                            key_max(u + 1, f, n % AXB)
                        if nxt and kind == "bias":
                            subtract_max(u + 1, f, n % AXB)
                        n += 1

            def first(u, layer):
                fills(u - 1, False, True)

            def phase(u, h, b, prev, nxt, nxt2):
                if prev:
                    sums_out(u)
                fills(u, prev, nxt)

            def last(u):
                sums_out(u)
                for f in range(AXB):
                    reciprocal(u, f)

            with dve.Fori(0, LAYERS) as layer:
                links = [0]

                def link(ins):
                    links[0] += 1
                    ins.then_inc(gn_link, 1)
                    dve.wait_ge(gn_link, layer * GN_LINKS + links[0])

                for t in range(2):
                    for b in range(IMAGES):
                        for s in range(GRP):
                            i = dve.bn_stats(stats[:, 2 * t + b, s, :],
                                             x[:, t, b * N + s * BLK:b * N + (s + 1) * BLK])
                dve.wait_ge(weights_in, (layer + 1) * 11 * 16)
                link(i)
                dve.tensor_tensor(bqks[:, :], bqk[:, :], qkscale[:, :], ALU.mult)
                for i in range(4):
                    last_ = dve.bn_aggr(mv[:, i, :], stats[:, i, :, :])
                last_.then_inc(gn_ready, 1)
                dve.wait_ge(gn_ready, layer * 3 + 1)
                dve.wait_ge(gn_sum, layer * 2 + 1)
                link(dve.tensor_copy(gm[:, :], aux[0:HALF, 0, 0:4]))
                link(dve.tensor_tensor(gt[:, :], mv[:, :, 0], gm[:, :], ALU.subtract))
                link(dve.tensor_tensor(gt[:, :], gt[:, :], gt[:, :], ALU.mult))
                dve.tensor_tensor(gv[:, :], gt[:, :], mv[:, :, 1], ALU.add).then_inc(gn_ready, 1)
                dve.wait_ge(gn_sum, layer * 2 + 2)
                dve.tensor_scalar(gv[:, :], aux[0:HALF, 0, 0:4], EPS, None, ALU.add).then_inc(gn_ready, 1)
                dve.wait_ge(gn_root, layer + 1)
                dve.wait_ge(gn_ready, layer * 3 + 3)
                link(dve.reciprocal(gr[:, :], gs[:, :]))
                link(dve.tensor_tensor(gt[:, :], gr[:, :], gr[:, :], ALU.mult))
                link(dve.tensor_tensor(gt[:, :], gt[:, :], gv[:, :], ALU.mult))
                link(dve.tensor_scalar(gt[:, :], gt[:, :], -0.5, 1.5, ALU.mult, ALU.add))
                link(dve.tensor_tensor(gr[:, :], gr[:, :], gt[:, :], ALU.mult))
                link(dve.scalar_tensor_tensor(out=gn[:, :], in0=gm[:, :], scalar=-1.0, in1=gr[:, :],
                                              op0=ALU.mult, op1=ALU.mult))
                link(dve.tensor_copy(tab[:, :, :], tabf[:, :, :]))
                link(dve.tensor_tensor(tabh[:, :, :], tabf[:, :, :], tab[:, :, :].bitcast(F32), ALU.subtract))
                link(dve.tensor_scalar(tabh[:, :, :], tabh[:, :, :], hlmask[:, 1:2], None, ALU.mult))
                link(dve.scalar_tensor_tensor(out=tab[:, :, :], in0=tab[:, :, :].bitcast(F32),
                                              scalar=hlmask[:, 0:1], in1=tabh[:, :, :],
                                              op0=ALU.mult, op1=ALU.add))
                assert links[0] == GN_LINKS
                for b in range(IMAGES):
                    for t in range(2):
                        i = 2 * t + b
                        dve.tensor_scalar(xn[:, t, b * N:(b + 1) * N], x[:, t, b * N:(b + 1) * N], gr[:, i:i + 1],
                                          gn[:, i:i + 1], ALU.mult, ALU.add).then_inc(xn_ready, 1)
                run_units(dve, layer, first, phase, last)
                for f in range(PJF):
                    m, blk = divmod(f, PJF // 2)
                    cols = slice(blk * SBW, (blk + 1) * SBW)
                    xs = x[:, m, cols].rearrange("p (a q) -> p a q", a=2)
                    dve.wait_ge(pj_filled, layer * PJF + f + 1)
                    dve.scalar_tensor_tensor(out=xs, in0=proj[0:HALF, f % 2, :, 0:BLK], scalar=bproj[:, m:m + 1],
                                             in1=xs, op0=ALU.add, op1=ALU.add).then_inc(pj_read, 1)
                dve.wait_ge(pj_read, (layer + 1) * PJF)

        @block.tensor
        def _(pe):
            pe.sem_inc(score_read, SCB)
            pe.sem_inc(slot_free, SLOTS)
            pe.wait_ge(const_in, 16 * 9)
            pe.wait_ge(const_set, 5)

            def fill_aux(j, b, kind, f, n):
                bank = aux[:, n % AXB, :]
                if kind == "relw":
                    for i in range(8):
                        w = 8 * f + i
                        mm = pe.matmul(bank[0:RELW, SIDE * i:SIDE * (i + 1)], tab[:, 1, SIDE - 1 - w:SIDE - 1 - w + RELW],
                                       qkhl[:, w:N:SIDE], start=True, stop=True)
                    mm.then_inc(rel_filled, 1)
                elif kind == "relh":
                    for i in range(8):
                        h = 8 * f + i
                        mm = pe.matmul(bank[0:RELW, SIDE * i:SIDE * (i + 1)], tab[:, 0, SIDE - 1 - h:SIDE - 1 - h + RELW],
                                       qkhl[:, SIDE * h:SIDE * (h + 1)], start=True, stop=True)
                    mm.then_inc(rel_filled, 1)
                elif kind == "max":
                    t, m = divmod(f, MAXB)
                    if f == 0:
                        pe.wait_ge(key_in, 32 * (j + 1))
                    if t % QG == 0 and m == 0:
                        pe.wait_ge(first_hi, j * GRP + t // QG + 1)
                    w = min(512, N - 512 * m)
                    pe.matmul(bank[:, 0:w], hi[:, b, t * P:(t + 1) * P], keys[:, b, 512 * m:512 * m + w],
                              start=True, stop=True).then_inc(max_filled, 1)
                else:
                    pe.wait_ge(diag_ready, j * GRP + f + 1)
                    pe.matmul(bank[:, 0:BLK], rowsel[:, :], diag[:, f % 2, :, :].rearrange("p t q -> p (t q)"),
                              start=True, stop=True).then_inc(bias_filled, 1)

            def read(j, kind, f, n):
                if kind in ("relw", "relh"):
                    pe.wait_ge(rel_read, j * REL + n + 1)
                elif kind == "max":
                    pe.wait_ge(max_read, j * MAXF + f + 1)
                else:
                    pe.wait_ge(bias_read, j * GRP + f + 1)

            order = [x_ for fills in plan for x_ in fills if x_[0] != "norm"]

            def norm_fill(u, f):
                if f == 0:
                    pe.wait_ge(o_read, u)
                pe.matmul(aux[:, f, 0:NRM], densel[:, :],
                          oraw[:, :, :].rearrange("p a q -> p (a q)")[:, f * NRM:(f + 1) * NRM],
                          start=True, stop=True).then_inc(norm_filled, 1)

            def attend(u, b, c, a_):
                if c == 0 and a_ == 0:
                    pe.wait_ge(vu_ready, u + 1)
                    pe.wait_ge(o_read, u)
                if a_ == 0:
                    pe.wait_ge(score_read, u * NSB + SB * (c + 1) + SCB)
                for j in range(4):
                    q = j * QUART + a_ * OH
                    mm = pe.matmul(out_ps[32 * j:32 * j + 32, a_, 0:OH], vu[:, b, c, :],
                                   probs[:, (KT * b + c) % SLOTS, q:q + OH], start=(c == 0), stop=(c == KT - 1))
                if a_ == 1:
                    mm.then_inc(slot_free, 1)

            def aux_fills(u, b, items, n, prev, nxt):
                for kind, f in items:
                    if kind == "norm":
                        if prev and nxt:
                            read(u + 1, *order[n - AXB + f], n - AXB + f)
                        elif prev:
                            read(u, *order[f - AXB], len(order) + f - AXB)
                        if prev:
                            norm_fill(u, f)
                        continue
                    if not nxt:
                        continue
                    if prev and REL <= n < REL + AXB:
                        pe.wait_ge(norm_read, AXB * (u - 1) + n - REL + 1)
                    elif n >= AXB:
                        read(u + 1, *order[n - AXB], n - AXB)
                    elif prev is not None:
                        read(u, *order[n - AXB], len(order) + n - AXB)
                    fill_aux(u + 1, 1 - b, kind, f, n)
                    n += 1
                return n

            def first(u, layer):
                pe.wait_ge(split, u + 1)
                n = 0
                for items in plan:
                    n = aux_fills(u - 1, 1, items, n, None, True)

            def phase(u, h, b, prev, nxt, nxt2):
                n = 0
                for k in range(NSB):
                    c, s = divmod(k, SB)
                    if c == 0:
                        pe.wait_ge(lo_ready, u * GRP + s + 1)
                    pe.wait_ge(score_read, u * NSB + k + 1)
                    for part in (hi, lo):
                        mm = pe.matmul(score[:, k % SCB, 0:BLK], keys[:, b, c * P:(c + 1) * P],
                                       part[:, b, s * BLK:(s + 1) * BLK], start=(part is hi), stop=(part is lo))
                    mm.then_inc(score_filled, 1)
                    if k == 0 and nxt:
                        pe.wait_ge(split, u + 2)
                    n = aux_fills(u, b, plan[k], n, prev, nxt)
                    if s in ATTEND_AT:
                        bank = ATTEND_AT.index(s)
                        if c:
                            attend(u, b, c - 1, bank)
                        elif prev:
                            attend(u - 1, 1 - b, KT - 1, bank)

            def last(u):
                for a_ in range(2):
                    attend(u - 1, 1, KT - 1, a_)
                for f in range(AXB):
                    pe.wait_ge(norm_read, AXB * (u - 1))
                    norm_fill(u, f)

            with pe.Fori(0, LAYERS) as layer:
                pe.wait_ge(gn_ready, layer * 3 + 1)
                pe.matmul(aux[0:HALF, 0, 0:4], gmat[:, :], mv[:, :, 0], start=True, stop=True).then_inc(gn_sum, 1)
                pe.wait_ge(gn_ready, layer * 3 + 2)
                pe.matmul(aux[0:HALF, 0, 0:4], gmat[:, :], gv[:, :], start=True, stop=True).then_inc(gn_sum, 1)
                for f in range(QKF):
                    k, s = divmod(f, PF)
                    b, m = divmod(k, 3)
                    if m == 0 and s == 0:
                        pe.wait_ge(xn_ready, layer * 4 + 2 * b + 2)
                    if f >= 2:
                        pe.wait_ge(qk_read, layer * (QKF + VF) + f - 1)
                    for a_ in range(2):
                        q = b * N + s * SBW + a_ * BLK
                        for t in range(2):
                            mm = pe.matmul(proj[:, f % 2, a_, 0:BLK], wqkv[:, t, m * P:(m + 1) * P], xn[:, t, q:q + BLK],
                                           start=(t == 0), stop=(t == 1))
                    mm.then_inc(qk_filled, 1)
                for v in range(VF):
                    f = QKF + v
                    pe.wait_ge(qk_read, layer * (QKF + VF) + f - 1)
                    for i in range(4):
                        to = proj[:, f % 2, i // 2, (i % 2) * CH:(i % 2 + 1) * CH]
                        tok = (4 * v + i) * P
                        pe.matmul(to, ones[:, :], bv[:, :], start=True, stop=False)
                        for t in range(2):
                            mm = pe.matmul(to, xn[:, t, tok:tok + P], wqkv[:, t, 2 * CH:3 * CH],
                                           start=False, stop=(t == 1))
                    mm.then_inc(qk_filled, 1)
                pe.wait_ge(qk_read, (layer + 1) * (QKF + VF))
                run_units(pe, layer, first, phase, last)
                pe.wait_ge(o_loaded, 32 * (layer + 1))
                for f in range(PJF):
                    m, blk = divmod(f, PJF // 2)
                    if f >= 2:
                        pe.wait_ge(pj_read, layer * PJF + f - 1)
                    else:
                        pe.wait_ge(score_read, (layer + 1) * UNITS * NSB + SCB)
                    for a_ in range(2):
                        q = blk * SBW + a_ * BLK
                        for t in range(2):
                            mm = pe.matmul(proj[0:HALF, f % 2, a_, 0:BLK], wproj[:, t, m * HALF:(m + 1) * HALF],
                                           xn[:, t, q:q + BLK], start=(t == 0), stop=(t == 1))
                    mm.then_inc(pj_filled, 1)


def kernel(**inputs):
    import numpy as np
    import concourse.bacc as bacc
    from concourse.bass_utils import run_bass_kernel_spmd

    names = [("L0_conv_", "qkv_w", "proj_w", "proj_b"), ("L1_conv_", "qkv_w", "proj_w", "proj_b"),
             ("L2_conv_", "qkv_w", "proj_w", "proj_b"), ("L3_conv_", "Wqkv", "Wproj", "bproj")]
    get = lambda n: np.asarray(inputs[n])
    wqkv = np.stack([get(p + q) for p, q, _, _ in names])
    wproj = np.stack([get(p + w) for p, _, w, _ in names])
    bproj = np.stack([get(p + v).reshape(2, HALF).T for p, _, _, v in names])
    bqkv = np.stack([get(p + "qkv_b") if p + "qkv_b" in inputs else np.zeros(3 * CH, np.float32)
                     for p, _, _, _ in names])
    rel = np.zeros((LAYERS, DH, 2, TBW), np.float32)
    for layer, (p, _, _, _) in enumerate(names):
        for d, (name, pad) in enumerate((("rel_pos_h", 0), ("rel_pos_w", 64))):
            r = get(p + name)
            take = np.minimum(np.arange(2 * SIDE - 2, -1, -1), r.shape[0] - 1)
            rel[layer, :, d, pad:pad + 2 * SIDE - 1] = r[take].T
    key = np.arange(N)
    onehot = np.zeros((P, N), np.float32)
    onehot[key // SIDE, key] = 1.0
    onehot[64 + key % SIDE, key] = 1.0
    rowsel = np.zeros((P, P), np.float32)
    rowsel[:, 0:SIDE] = 1.0
    densel = np.zeros((P, P), np.float32)
    for j in range(4):
        densel[32 * j + DH, 32 * j:32 * j + 32] = 1.0
    per = CH // GROUPS
    ch = np.arange(HALF) // per
    gmat = (ch[:, None] == ch[None, :]).astype(np.float32) / np.float32(per)
    part = np.arange(P) % 64
    hlmask = np.stack([part < 16, (part >= 16) & (part < 32)], axis=1).astype(np.float32)
    chan = np.arange(3 * P).reshape(3, P).T
    qkscale = np.where(chan < CH, 1.0, float(DH) ** -0.5).astype(np.float32)
    arrays = {
        "x": get("x").reshape(TOK, CH).T, "wqkv0": wqkv[:, 0:HALF], "wqkv1": wqkv[:, HALF:],
        "wproj0": wproj[:, 0:HALF], "wproj1": wproj[:, HALF:], "bproj": bproj,
        "bqk": bqkv[:, 0:2 * CH].reshape(LAYERS, 3, P).transpose(0, 2, 1), "bv": bqkv[:, None, 2 * CH:],
        "rel": rel, "key_onehot": onehot, "ident": np.eye(P, dtype=np.float32), "rowsel": rowsel,
        "densel": densel, "gmat": gmat, "hlmask": hlmask, "qkscale": qkscale,
    }
    arrays = {n: np.ascontiguousarray(v) for n, v in arrays.items()}
    nc = bacc.Bacc("TRN2", target_bir_lowering=False, num_devices=1)
    a = {n: nc.dram_tensor(f"in_{n}", v.shape, mybir.dt.from_np(v.dtype), kind="ExternalInput").ap()
         for n, v in arrays.items()}
    a["out"] = nc.dram_tensor("out_x", (CH, TOK), F32, kind="ExternalOutput").ap()
    build(nc, a)
    r = run_bass_kernel_spmd(nc, [{f"in_{n}": v for n, v in arrays.items()}], core_ids=[0])
    out = r.results[0]["out_x"]
    return np.ascontiguousarray(out.T).reshape(IMAGES, SIDE, SIDE, CH)
```

```python
from contextlib import ExitStack

import concourse.bass as bass
from concourse import mybir

F32 = mybir.dt.float32
F32R = mybir.dt.float32r
ACT = mybir.ActivationFunctionType
ALU = mybir.AluOpType
AX = mybir.AxisListType

LAYERS, IMAGES, SIDE, CH, HEADS = 4, 2, 48, 192, 12
GROUPS, EPS = 32, 1e-5
DH = CH // HEADS
N = SIDE * SIDE
TOK = IMAGES * N
HALF = CH // 2
UNITS = IMAGES * HEADS
P = 128
KT = N // P
HW = SIDE // 2
CPH = N // 2 // P
ROWS = 6
BLK = 384
GRP = N // BLK
QG = BLK // P
SBW = 2 * BLK
QB = N // SBW
PAIRS = QB * CPH
SCB = 3
AXB = 4
NSB = 4 * PAIRS
SLOTS = 6
QUART = SBW // 4
TBW = 2 * SIDE
MAXB = 5
REL = 2 * GRP
MAXF = KT * MAXB
PF = N // SBW
QKF = IMAGES * 3 * PF
VF = TOK // P // 4
PJF = 2 * TOK // SBW
SPLIT_AT = 72
COMMON = 8
KEY_LOAD = {1: (0, 1), 2: (2,), 3: (3,)}
REP_LOAD = {4: (0,), 5: (1,), 6: (2,), 9: (3, 4, 5), 10: (6, 7)}
OUT_AT = 11
SUMS_AT = 3
RING = 3
REL_ORDER = [("relw", 0), ("relw", 1), ("relw", 2)] + [("relh", r) for r in range(GRP)] \
    + [("relw", 3), ("relw", 4), ("relw", 5)]
REL_FIRST = 6
REL_BEHIND = {3: 6, 6: 7, 9: 8, 14: 9, 18: 10, 22: 11}
NORM_AT = 8
TAIL = 3
FIRST_HIGH = {("relh", 1): 0, ("relh", 3): 1, ("relh", 5): 2, ("max", 26): 3, ("max", 32): 4, ("max", 38): 5}
GN_LINKS = 14


def schedule():
    seq = []
    for g in range(GRP):
        for k in range(QG * MAXB):
            f = g * QG * MAXB + k
            seq.append([("max", f)])
            if f in REL_BEHIND:
                seq.append([REL_ORDER[REL_BEHIND[f]]])
            if g and k == 9:
                seq.append([("bias", g - 1)])
    seq.append([("bias", GRP - 1)])
    seq = [[r] for r in REL_ORDER[:REL_FIRST]] + seq
    seq[NORM_AT:NORM_AT] = [[("norm", f)] for f in range(QB)]
    head, rest = seq[:NORM_AT + QB], [i[0] for i in seq[NORM_AT + QB:]]
    places = NSB - len(head) - TAIL
    cuts = [-(-len(rest) * k // places) for k in range(places + 1)]
    return head + [rest[cuts[k]:cuts[k + 1]] for k in range(places)] + [[]] * TAIL


def build(nc, a):
    plan = schedule()
    with ExitStack() as ctx:
        def sb(name, shape, dt=F32):
            return ctx.enter_context(nc.sbuf_tensor(name, shape, dt))

        def ps(name, shape):
            return ctx.enter_context(nc.psum_tensor(name, shape, F32))

        def sem(name):
            return ctx.enter_context(nc.semaphore(name))

        qk_dram = nc.dram_tensor("qk_scratch", (2 * CH, TOK), F32).ap()
        ao_dram = nc.dram_tensor("attention_scratch", (CH, TOK), F32).ap()

        x_dram = nc.dram_tensor("x_scratch", (CH, TOK), F32).ap()

        region = sb("region", [P, 2 * TOK])
        xn = region[0:HALF, :].rearrange("p (t n) -> p t n", t=2)
        probs = region[:, :].rearrange("p (s n) -> p s n", s=2 * SLOTS)
        vall = sb("vall", [P, TOK // P, CH])
        vu = sb("vu", [P, 2, KT, 32])
        full = sb("full", [P, N])
        qkrep = sb("qkrep", [P, N])
        qkhl = sb("qkhl", [P, N], F32R)
        hi = sb("hi", [P, 2, N], F32R)
        lo = sb("lo", [P, 2, N], F32R)
        mkeys = sb("mkeys", [P, N], F32R)
        keys = sb("keys", [P, 2, N], F32R)
        moving = sb("moving", [P, 2, RING, 2, SBW], F32R)
        wproj = sb("wproj", [HALF, 2, CH])
        tab = sb("tab", [P, 2, TBW], F32R)
        ident = sb("ident", [P, P])
        rowsel = sb("rowsel", [P, P], F32R)
        densel = sb("densel", [P, P])
        gmat = sb("gmat", [HALF, HALF])
        hlmask = sb("hlmask", [P, 2])
        qkscale = sb("qkscale", [P, 3])
        bqk = sb("bqk", [P, 3])
        bqks = sb("bqks", [P, 3])
        ones = sb("ones", [1, P])
        bproj = sb("bproj", [HALF, 2])
        mpart = sb("mpart", [P, 2, QG, MAXB])
        mcol = sb("mcol", [P, 2, QG])
        diag = sb("diag", [P, 2, QG, P], F32R)
        oraw = sb("oraw", [P, QB, QUART])
        orec = sb("orec", [P, QB, QUART])
        start = lo[:, :, :].rearrange("p b n -> p (b n)").bitcast(F32)
        wqkv = start[0:HALF, 0:6 * CH].rearrange("p (t c) -> p t c", t=2)
        bv = start[0:1, 6 * CH:7 * CH]
        tabf, tabh = (start[:, 7 * CH + i * 2 * TBW:7 * CH + (i + 1) * 2 * TBW].rearrange("p (d k) -> p d k", d=2)
                      for i in range(2))
        stats = start[0:HALF, 7 * CH + 4 * TBW:7 * CH + 4 * TBW + 4 * GRP * 6].rearrange("p (i s k) -> p i s k", i=4, k=6)
        mv = sb("mv", [HALF, 4, 2])
        gm = sb("gm", [HALF, 4])
        gt = sb("gt", [HALF, 4])
        gv = sb("gv", [HALF, 4])
        gs = sb("gs", [HALF, 4])
        gr = sb("gr", [HALF, 4])
        gn = sb("gn", [HALF, 4])

        work = ps("work", [P, SCB + AXB, 512])
        score = work[:, 0:SCB, :]
        aux = work[:, SCB:SCB + AXB, :]
        proj = work[:, 0:4, :].rearrange("p (f a) q -> p f a q", a=2)
        out_ps = ps("out_ps", [P, 512])

        const_in = sem("const_in")
        x_copied = sem("x_copied")
        x_in = sem("x_in")
        piece_in = [sem("piece_in_full"), sem("piece_in_rep")]
        piece_out = [sem("piece_out_full"), sem("piece_out_rep")]
        weights_in = sem("weights_in")
        const_set = sem("const_set")
        pool_set = sem("pool_set")
        gn_link = sem("gn_link")
        gn_sum = sem("gn_sum")
        gn_ready = sem("gn_ready")
        gn_root = sem("gn_root")
        xn_ready = sem("xn_ready")
        qk_filled = sem("qk_filled")
        qk_read = sem("qk_read")
        qk_stored = [sem("qk_stored_full"), sem("qk_stored_rep")]
        rep_in = sem("rep_in")
        full_in = [sem("full_in_0"), sem("full_in_1")]
        split_high = sem("split_high")
        split = sem("split")
        key_in = sem("key_in")
        skey_in = sem("skey_in")
        common_in = [sem("common_in_0"), sem("common_in_1")]
        row_in = [[sem(f"row_in_{p}{s}") for s in range(RING)] for p in range(2)]
        vu_ready = sem("vu_ready")
        rel_filled = sem("rel_filled")
        rel_read = sem("rel_read")
        first_hi = sem("first_hi")
        max_filled = sem("max_filled")
        max_read = sem("max_read")
        mx_link = sem("mx_link")
        diag_ready = sem("diag_ready")
        bias_filled = sem("bias_filled")
        bias_read = sem("bias_read")
        hi_ready = sem("hi_ready")
        lo_ready = sem("lo_ready")
        score_filled = sem("score_filled")
        score_read = sem("score_read")
        slot_free = sem("slot_free")
        o_read = sem("o_read")
        norm_filled = sem("norm_filled")
        norm_read = sem("norm_read")
        o_ready = sem("o_ready")
        o_stored = sem("o_stored")
        o_loaded = sem("o_loaded")
        pj_filled = sem("pj_filled")
        pj_read = sem("pj_read")
        stored = sem("stored")

        def run_units(eng, layer, first, phase, last):
            base = layer * UNITS
            pair = layer * HEADS
            first(eng.snap(base), eng.snap(pair), layer)
            phase(eng.snap(base), eng.snap(pair), 0, 0, False, True, True)
            with eng.Fori(0, HEADS - 2) as h:
                phase(eng.snap(base + h * 2 + 1), eng.snap(pair + h), h, 1, True, True, True)
                phase(eng.snap(base + h * 2 + 2), eng.snap(pair + h + 1), h + 1, 0, True, True, True)
            phase(eng.snap(base + UNITS - 3), eng.snap(pair + HEADS - 2), HEADS - 2, 1, True, True, True)
            phase(eng.snap(base + UNITS - 2), eng.snap(pair + HEADS - 1), HEADS - 1, 0, True, True, False)
            phase(eng.snap(base + UNITS - 1), eng.snap(pair + HEADS - 1), HEADS - 1, 1, True, False, False)
            last(eng.snap(base + UNITS))

        block = ctx.enter_context(nc.Block())

        @block.sync
        def _(sp):
            for dst, name in ((full[:, :], "max_onehot"), (qkrep[:, :], "key_onehot"), (region[:, 0:P], "rowsel"),
                              (ident[:, :], "ident"), (densel[:, :], "densel"), (gmat[:, :], "gmat"),
                              (hlmask[:, :], "hlmask"), (qkscale[:, :], "qkscale")):
                sp.dma_start(dst, a[name]).then_inc(const_in, 16)
            sp.dma_start(x_dram, a["x"]).then_inc(x_copied, 16)
            sp.wait_ge(x_copied, 16)

            def settle():
                sp.wait_ge(const_set, 6)

            def rep_load(h, b, i):
                k = i // 2 % 2
                sp.dma_start(qkrep[i * DH:(i + 1) * DH, :],
                             qk_dram[bass.ds(h * DH + k * CH, DH), b * N:(b + 1) * N]).then_inc(rep_in, 16)

            def full_load(h, b, half):
                for p in (48, 112):
                    sp.dma_start(full[p:p + DH, half * N // 2:(half + 1) * N // 2],
                                 qk_dram[bass.ds(h * DH, DH), b * N + half * N // 2:b * N + (half + 1) * N // 2])\
                      .then_inc(full_in[half], 16)

            def max_key_load():
                for p, src in ((48, 32), (112, 96)):
                    sp.dma_start(mkeys[p:p + DH, :].bitcast(F32), qkhl[src:src + DH, :].bitcast(F32)).then_inc(key_in, 16)

            def key_load(b, r):
                src = (32, 96, 48, 112)[r]
                sp.dma_start(keys[64 + r * DH:64 + (r + 1) * DH, b, :].bitcast(F32),
                             qkhl[src:src + DH, :].bitcast(F32)).then_inc(skey_in, 16)

            def row_load(b, qb, c):
                par, cols, h0 = (QB * b + qb) % 2, slice(qb * SBW, (qb + 1) * SBW), c * P // HW
                for p, part in ((0, hi), (ROWS, lo)):
                    src = part[h0:h0 + ROWS, b, cols].bitcast(F32)
                    sp.dma_start(moving[p:p + ROWS, par, c % RING, :, :].bitcast(F32),
                                 src.unsqueeze(1).broadcast_to((ROWS, 2, SBW))).then_inc(row_in[par][c % RING], 16)

            def common_load(b, qb, i):
                par, cols = (QB * b + qb) % 2, slice(qb * SBW, (qb + 1) * SBW)
                if i < 4:
                    p, src, part = ((64, 48, hi), (80, 112, hi), (96, 48, lo), (112, 112, lo))[i]
                    sp.dma_start(moving[p:p + DH, par, :, :, :].rearrange("p s a q -> p (s a) q").bitcast(F32),
                                 part[src:src + DH, b, cols].bitcast(F32).unsqueeze(1).broadcast_to((DH, 2 * RING, SBW)))\
                      .then_inc(common_in[par], 16)
                else:
                    a_ = i % 2
                    p, part = ((16, hi), (16 + HW, lo))[i // 2 - 2]
                    sp.dma_start(moving[p:p + HW, par, :, a_, :].bitcast(F32),
                                 part[64 + a_ * HW:64 + (a_ + 1) * HW, b, cols].bitcast(F32)
                                 .unsqueeze(1).broadcast_to((HW, RING, SBW))).then_inc(common_in[par], 16)

            def first(u, v, layer):
                for stored_from in qk_stored:
                    sp.wait_ge(stored_from, (layer + 1) * 3 * 16)
                for i in range(8):
                    rep_load(0, 0, i)
                for half in range(2):
                    full_load(0, 0, half)
                sp.wait_ge(split, u + 1)
                max_key_load()
                for r in range(4):
                    key_load(0, r)
                for i in range(8):
                    rep_load(0, 1, i)
                sp.wait_ge(lo_ready, u * GRP + 2)
                for i in range(COMMON):
                    common_load(0, 0, i)
                row_load(0, 0, 0)
                sp.wait_ge(split, u + 2)
                row_load(0, 0, 1)

            def out_store(u, h, b, j):
                if j == 0:
                    sp.wait_ge(o_ready, u)
                    settle()
                to = ao_dram[bass.ds(h * DH, DH), b * N:(b + 1) * N].rearrange("p (a j q) -> p a j q", a=QB, j=4)
                sp.dma_start(to[:, :, j, :], orec[32 * j:32 * j + DH, :, :]).then_inc(o_stored, 16)

            def phase(u, v, h, b, prev, nxt, nxt2):
                for e in range(PAIRS):
                    qb, c = divmod(e, CPH)
                    if e == 0:
                        sp.wait_ge(lo_ready, (u + 1) * GRP - 1)
                    elif c == 0 and (nxt or qb + 1 < QB):
                        sp.wait_ge(lo_ready, (u + 1) * GRP if qb + 1 < QB else (u + 1) * GRP + 2)
                    if c == 0:
                        row_load(b, qb, 2)
                    if e == 0 and nxt:
                        full_load(h + b, 1 - b, 0)
                        sp.wait_ge(max_read, (u + 1) * MAXF)
                        max_key_load()
                    if e == 1:
                        sp.wait_ge(score_filled, u * NSB + 1)
                    elif c and (nxt or e < PAIRS - CPH + 1 or 2 <= c < CPH - 1):
                        sp.wait_ge(score_filled, u * NSB + 4 * (e - 1))
                    if 2 <= c < CPH - 1:
                        row_load(b, qb, c + 1)
                    if e == 2 and nxt:
                        sp.wait_ge(lo_ready, (u + 1) * GRP)
                        full_load(h + b, 1 - b, 1)
                    if c >= 1:
                        if qb + 1 < QB:
                            common_load(b, qb + 1, c - 1)
                        elif nxt:
                            common_load(1 - b, 0, c - 1)
                    if c in (1, CPH - 1):
                        if qb + 1 < QB:
                            row_load(b, qb + 1, 0 if c == 1 else 1)
                        elif nxt:
                            row_load(1 - b, 0, 0 if c == 1 else 1)
                    if nxt and e in KEY_LOAD:
                        for r in KEY_LOAD[e]:
                            key_load(1 - b, r)
                    if nxt2 and e in REP_LOAD:
                        for i in REP_LOAD[e]:
                            rep_load(h + 1, b, i)
                    if prev and 0 <= e - OUT_AT < 4:
                        out_store(u, h - 1 + b, 1 - b, e - OUT_AT)

            def last(u):
                for j in range(4):
                    out_store(u, HEADS - 1, 1, j)

            with sp.Fori(0, LAYERS) as layer:
                def weight(dst, name):
                    letters = " ".join("abcd"[:len(a[name].shape) - 2])
                    src = a[name][bass.ds(layer, 1)].rearrange(f"o p {letters} -> (o p) {letters}")
                    sp.dma_start(dst, src).then_inc(weights_in, 16)

                sp.wait_ge(const_set, 6)
                for t in (1, 0):
                    sp.wait_ge(piece_out[t], layer * 32)
                    sp.dma_start(xn[:, t, :], x_dram[t * HALF:(t + 1) * HALF, :]).then_inc(x_in, 16)
                weight(wqkv[:, 0, :], "wqkv0")
                weight(wqkv[:, 1, :], "wqkv1")
                weight(wproj[:, 0, :], "wproj0")
                weight(wproj[:, 1, :], "wproj1")
                weight(bqk[:, :], "bqk")
                weight(bv[:, :], "bv")
                weight(bproj[:, :], "bproj")
                weight(tabf[:, :, :], "rel")
                for k in range(IMAGES * 3):
                    b, m = divmod(k, 3)
                    sp.wait_ge(qk_read, layer * (QKF + VF) + PF * (k + 1))
                    sp.dma_start(qk_dram[m * P:(m + 1) * P, b * N:(b + 1) * N],
                                 (full, qkrep)[k % 2][:, :]).then_inc(qk_stored[k % 2], 16)
                run_units(sp, layer, first, phase, last)
                sp.wait_ge(o_stored, (layer + 1) * UNITS * 64)
                for t in range(2):
                    sp.dma_start(xn[:, t, :], ao_dram[t * HALF:(t + 1) * HALF, :]).then_inc(o_loaded, 16)
                def piece(i):
                    return x_dram[(i % 2) * HALF:(i % 2 + 1) * HALF, i // 2 * N:(i // 2 + 1) * N]

                for i in range(4):
                    if i >= 2:
                        sp.wait_ge(piece_out[i % 2], (layer * 2 + i // 2) * 16)
                    sp.dma_start((full, qkrep)[i % 2][0:HALF, :], piece(i)).then_inc(piece_in[i % 2], 16)
                    if i >= 1:
                        sp.wait_ge(pj_read, layer * PJF + PF * i)
                        sp.dma_start(piece(i - 1), (full, qkrep)[(i - 1) % 2][0:HALF, :])\
                          .then_inc(piece_out[(i - 1) % 2], 16)
                sp.wait_ge(pj_read, (layer + 1) * PJF)
                sp.dma_start(piece(3), qkrep[0:HALF, :]).then_inc(piece_out[1], 16)
            for i in range(2):
                sp.wait_ge(piece_out[i], LAYERS * 32)
            sp.dma_start(a["out"], x_dram).then_inc(stored, 16)
            sp.wait_ge(stored, 16)

        @block.gpsimd
        def _(pool):
            pool.memset(vu[:, :, :, DH:32], 0.0).then_inc(pool_set, 1)
            pool.wait_ge(pool_set, 1)
            pool.memset(vu[:, :, :, DH:DH + 1], 1.0).then_inc(pool_set, 1)
            pool.wait_ge(pool_set, 2)

            def split_low(j):
                pool.wait_ge(split_high, j + 1)
                pool.tensor_tensor(qkhl[64:128, :], qkrep[64:128, :], qkhl[64:128, :].bitcast(F32),
                                   ALU.subtract).then_inc(split, 1)

            def values(b, h):
                pool.tensor_copy(vu[:, b, :, 0:DH],
                                 vall[:, b * KT:(b + 1) * KT, bass.ds(h * DH, DH)]).then_inc(vu_ready, 1)

            def prepare(j, h, b, split_next):
                for g in range(GRP):
                    cols = slice(g * BLK, (g + 1) * BLK)
                    if g == 0:
                        pool.wait_ge(split, j + 1)
                    if g == 4 and split_next:
                        pool.wait_ge(split, j + 2)
                    pool.wait_ge(hi_ready, j * GRP + g + 1)
                    pool.tensor_tensor(lo[:, b, cols], full[:, cols], hi[:, b, cols].bitcast(F32),
                                       ALU.subtract).then_inc(lo_ready, 1)
                    if g == 0:
                        values(b, h)
                    if g == 3 and split_next:
                        pool.wait_ge(lo_ready, j * GRP + 4)
                        split_low(j + 1)

            def first(u, v, layer):
                pool.wait_ge(qk_read, (layer + 1) * (QKF + VF))
                split_low(u)
                prepare(u, 0, 0, False)
                pool.wait_ge(lo_ready, (u + 1) * GRP)
                split_low(u + 1)

            def normalise(u):
                pool.wait_ge(norm_read, QB * u)
                pool.tensor_tensor(orec[:, :, :], oraw[:, :, :], orec[:, :, :], ALU.mult).then_inc(o_ready, 1)

            def phase(u, v, h, b, prev, nxt, nxt2):
                if prev:
                    pool.wait_ge(slot_free, u * PAIRS + SLOTS)
                    normalise(u)
                if nxt:
                    prepare(u + 1, h + b, 1 - b, nxt2)

            with pool.Fori(0, LAYERS) as layer:
                run_units(pool, layer, first, phase, normalise)

        @block.scalar
        def _(act):
            def rel_out(j, kind, r, n):
                i = REL_ORDER.index((kind, r))
                act.wait_ge(rel_filled, j * REL + i + 1)
                bank = aux[:, n % AXB, 0:BLK]
                if kind == "relh":
                    to = full[0:SIDE, :].rearrange("p (a h w) -> p a h w", a=2, w=HW)[:, :, 8 * r:8 * r + 8, :]
                    act.activation(to, bank[0:SIDE, :].rearrange("p (h a w) -> p a h w", a=2, w=HW), ACT.Copy)\
                       .then_inc(rel_read, 1)
                else:
                    to = full[64:64 + SIDE, :].rearrange("p (a h w) -> p a h w", a=2, w=HW)
                    to = to[:, r // 3, :, 8 * (r % 3):8 * (r % 3) + 8]
                    act.activation(to, bank[0:SIDE, :].rearrange("p (w h) -> p h w", w=8), ACT.Copy)\
                       .then_inc(rel_read, 1)

            def high(j, b, g, ready):
                cols = slice(g * BLK, (g + 1) * BLK)
                act.activation(hi[:, b, cols], full[:, cols], ACT.Copy).then_inc(ready, 1)

            def high_behind(j, b, kind, f):
                if (kind, f) in FIRST_HIGH:
                    g = FIRST_HIGH[kind, f]
                    before = REL if g >= GRP // 2 else REL_ORDER.index((kind, f)) + 1
                    act.wait_ge(rel_read, j * REL + before)
                    if g in (0, GRP // 2):
                        act.wait_ge(full_in[2 * g // GRP], 32 * (j + 1))
                    high(j, b, g, first_hi)
                elif kind == "bias":
                    act.wait_ge(bias_read, j * GRP + f + 1)
                    high(j, b, f, hi_ready)

            def split_qk(j):
                act.wait_ge(rep_in, 128 * (j + 1))
                act.activation(qkhl[:, :], qkrep[:, :], ACT.Copy).then_inc(split_high, 1)

            def first(u, v, layer):
                split_qk(u)
                n = 0
                for kind, f in [item for items in plan for item in items if item[0] != "norm"]:
                    if kind in ("relw", "relh"):
                        rel_out(u, kind, f, n)
                    high_behind(u, 0, kind, f)
                    n += 1
                act.wait_ge(key_in, 32 * (u + 1))
                act.wait_ge(skey_in, 64 * (u + 1))
                split_qk(u + 1)

            def phase(u, v, h, b, prev, nxt, nxt2):
                n, late = 0, []
                for k in range(NSB):
                    if k % 4 == 0:
                        act.wait_ge(slot_free, u * PAIRS + k // 4 + 1)
                    act.wait_ge(score_filled, u * NSB + k + 1)
                    act.activation(probs[:, (2 * PAIRS * b + k // 2) % (2 * SLOTS), k % 2 * BLK:(k % 2 + 1) * BLK],
                                   score[:, k % SCB, 0:BLK], ACT.Exp).then_inc(score_read, 1)
                    if not nxt:
                        continue
                    for f in late:
                        high_behind(u + 1, 1 - b, "bias", f)
                    late = [f for kind, f in plan[k] if kind == "bias"]
                    for kind, r in plan[k]:
                        if kind in ("relw", "relh"):
                            if kind == "relw" and r == 0:
                                act.wait_ge(lo_ready, u * GRP + 3)
                            if kind == "relh" and r == 0:
                                act.wait_ge(lo_ready, (u + 1) * GRP)
                            rel_out(u + 1, kind, r, n)
                        if kind != "bias":
                            high_behind(u + 1, 1 - b, kind, r)
                        n += kind != "norm"
                    if k == SPLIT_AT and nxt2:
                        act.wait_ge(key_in, 32 * (u + 2))
                        act.wait_ge(skey_in, 64 * (u + 2))
                        split_qk(u + 2)
                if nxt:
                    for f in late:
                        high_behind(u + 1, 1 - b, "bias", f)

            with act.Fori(0, LAYERS) as layer:
                act.wait_ge(gn_ready, layer * 3 + 3)
                act.activation(gs[:, :], gv[:, :], ACT.Sqrt).then_inc(gn_root, 1)
                for f in range(QKF):
                    k, s = divmod(f, PF)
                    if s == 0 and k >= 2:
                        act.wait_ge(qk_stored[k % 2], (layer * 3 + k // 2) * 16)
                    act.wait_ge(qk_filled, layer * (QKF + VF) + f + 1)
                    m = k % 3
                    to = (full, qkrep)[k % 2][:, s * SBW:(s + 1) * SBW].rearrange("p (a q) -> p a q", a=2)
                    act.activation(to, proj[:, f % 2, :, 0:BLK], ACT.Identity, bias=bqks[:, m:m + 1],
                                   scale=qkscale[:, m:m + 1]).then_inc(qk_read, 1)
                for v in range(VF):
                    f = QKF + v
                    act.wait_ge(qk_filled, layer * (QKF + VF) + f + 1)
                    act.activation(vall[:, 4 * v:4 * v + 4, :].rearrange("p (a t) c -> p a (t c)", a=2),
                                   proj[:, f % 2, :, 0:BLK], ACT.Copy).then_inc(qk_read, 1)
                run_units(act, layer, first, phase, lambda u: None)

        @block.vector
        def _(dve):
            dve.memset(ones[:, :], 1.0).then_inc(const_set, 1)
            dve.memset(moving[0:32, :, :, :, :].bitcast(F32), 0.0).then_inc(const_set, 1)
            dve.wait_ge(const_in, 16 * 8)
            dve.tensor_copy(mkeys[:, :], full[:, :]).then_inc(const_set, 1)
            for b in range(IMAGES):
                dve.tensor_copy(keys[:, b, :], qkrep[:, :]).then_inc(const_set, 1)
            dve.tensor_copy(rowsel[:, :], region[:, 0:P]).then_inc(const_set, 1)
            dve.wait_ge(const_set, 6)

            def key_max(j, f, bank):
                t, m = divmod(f, MAXB)
                g = t // QG
                w = min(512, N - 512 * m)
                dve.wait_ge(max_filled, j * MAXF + f + 1)
                dve.tensor_reduce(mpart[:, g % 2, t % QG, m:m + 1], aux[:, bank, 0:w], AX.X, ALU.max)\
                   .then_inc(max_read, 1)
                if f % (QG * MAXB) == QG * MAXB - 1:
                    dve.wait_ge(max_read, j * MAXF + f + 1)
                    dve.tensor_reduce(mcol[:, g % 2, :], mpart[:, g % 2, :, :], AX.X, ALU.max).then_inc(mx_link, 1)
                    dve.wait_ge(mx_link, j * GRP + g + 1)
                    for t in range(QG):
                        last = dve.tensor_scalar(diag[:, g % 2, t, :], ident[:, :], mcol[:, g % 2, t:t + 1], None,
                                                 ALU.mult)
                    last.then_inc(diag_ready, 1)

            def subtract_max(j, g, bank):
                cols = slice(g * BLK, (g + 1) * BLK)
                dve.wait_ge(bias_filled, j * GRP + g + 1)
                dve.tensor_tensor(full[:, cols], full[:, cols], aux[:, bank, 0:BLK], ALU.subtract)\
                   .then_inc(bias_read, 1)

            def sums_out(u, b, qb):
                dve.wait_ge(slot_free, u * PAIRS + (qb + 1) * CPH + SLOTS)
                if qb == 0:
                    dve.wait_ge(o_ready, u)
                dve.tensor_copy(oraw[:, qb, :], out_ps[:, 0:QUART]).then_inc(o_read, 1)

            def reciprocal(u, f):
                if f == 0:
                    dve.wait_ge(o_stored, 64 * (u - 1))
                dve.wait_ge(norm_filled, QB * (u - 1) + f + 1)
                dve.reciprocal(orec[:, f, :], aux[:, f, 0:QUART]).then_inc(norm_read, 1)

            def fills(u, prev, nxt):
                n = 0
                for k, items in enumerate(plan):
                    if prev is not None and k in (4 * CPH + SUMS_AT, 8 * CPH + SUMS_AT):
                        sums_out(u, 1 if prev == 2 else 0, k // (4 * CPH) - 1)
                    if prev and k == SUMS_AT:
                        sums_out(u - 1, 0 if prev == 2 else 1, QB - 1)
                    for kind, f in items:
                        if kind == "norm":
                            if prev:
                                reciprocal(u, f)
                            continue
                        if nxt and kind == "max":
                            key_max(u + 1, f, n % AXB)
                        if nxt and kind == "bias":
                            subtract_max(u + 1, f, n % AXB)
                        n += 1

            def first(u, v, layer):
                fills(u - 1, None, True)

            def phase(u, v, h, b, prev, nxt, nxt2):
                fills(u, prev and 1 + b, nxt)

            def last(u):
                sums_out(u - 1, 1, QB - 1)
                for f in range(QB):
                    reciprocal(u, f)

            with dve.Fori(0, LAYERS) as layer:
                links = [0]

                def link(ins):
                    links[0] += 1
                    ins.then_inc(gn_link, 1)
                    dve.wait_ge(gn_link, layer * GN_LINKS + links[0])

                dve.wait_ge(x_in, (layer + 1) * 32)
                for t in range(2):
                    for b in range(IMAGES):
                        for s in range(GRP):
                            i = dve.bn_stats(stats[:, 2 * t + b, s, :],
                                             xn[:, t, b * N + s * BLK:b * N + (s + 1) * BLK])
                dve.wait_ge(weights_in, (layer + 1) * 8 * 16)
                link(i)
                dve.tensor_tensor(bqks[:, :], bqk[:, :], qkscale[:, :], ALU.mult)
                for i in range(4):
                    last_ = dve.bn_aggr(mv[:, i, :], stats[:, i, :, :])
                last_.then_inc(gn_ready, 1)
                dve.wait_ge(gn_ready, layer * 3 + 1)
                dve.wait_ge(gn_sum, layer * 2 + 1)
                link(dve.tensor_copy(gm[:, :], aux[0:HALF, 0, 0:4]))
                link(dve.tensor_tensor(gt[:, :], mv[:, :, 0], gm[:, :], ALU.subtract))
                link(dve.tensor_tensor(gt[:, :], gt[:, :], gt[:, :], ALU.mult))
                dve.tensor_tensor(gv[:, :], gt[:, :], mv[:, :, 1], ALU.add).then_inc(gn_ready, 1)
                dve.wait_ge(gn_sum, layer * 2 + 2)
                dve.tensor_scalar(gv[:, :], aux[0:HALF, 0, 0:4], EPS, None, ALU.add).then_inc(gn_ready, 1)
                dve.wait_ge(gn_root, layer + 1)
                dve.wait_ge(gn_ready, layer * 3 + 3)
                link(dve.reciprocal(gr[:, :], gs[:, :]))
                link(dve.tensor_tensor(gt[:, :], gr[:, :], gr[:, :], ALU.mult))
                link(dve.tensor_tensor(gt[:, :], gt[:, :], gv[:, :], ALU.mult))
                link(dve.tensor_scalar(gt[:, :], gt[:, :], -0.5, 1.5, ALU.mult, ALU.add))
                link(dve.tensor_tensor(gr[:, :], gr[:, :], gt[:, :], ALU.mult))
                link(dve.scalar_tensor_tensor(out=gn[:, :], in0=gm[:, :], scalar=-1.0, in1=gr[:, :],
                                              op0=ALU.mult, op1=ALU.mult))
                link(dve.tensor_copy(tab[:, :, :], tabf[:, :, :]))
                link(dve.tensor_tensor(tabh[:, :, :], tabf[:, :, :], tab[:, :, :].bitcast(F32), ALU.subtract))
                link(dve.tensor_scalar(tabh[:, :, :], tabh[:, :, :], hlmask[:, 1:2], None, ALU.mult))
                link(dve.scalar_tensor_tensor(out=tab[:, :, :], in0=tab[:, :, :].bitcast(F32),
                                              scalar=hlmask[:, 0:1], in1=tabh[:, :, :],
                                              op0=ALU.mult, op1=ALU.add))
                assert links[0] == GN_LINKS
                for b in range(IMAGES):
                    for t in range(2):
                        i = 2 * t + b
                        dve.tensor_scalar(xn[:, t, b * N:(b + 1) * N], xn[:, t, b * N:(b + 1) * N], gr[:, i:i + 1],
                                          gn[:, i:i + 1], ALU.mult, ALU.add).then_inc(xn_ready, 1)
                run_units(dve, layer, first, phase, last)
                for f in range(PJF):
                    i, blk = divmod(f, PF)
                    xs = (full, qkrep)[i % 2][0:HALF, blk * SBW:(blk + 1) * SBW].rearrange("p (a q) -> p a q", a=2)
                    if blk == 0:
                        dve.wait_ge(piece_in[i % 2], (layer * 2 + i // 2 + 1) * 16)
                    dve.wait_ge(pj_filled, layer * PJF + f + 1)
                    dve.scalar_tensor_tensor(out=xs, in0=proj[0:HALF, f % 2, :, 0:BLK], scalar=bproj[:, i % 2:i % 2 + 1],
                                             in1=xs, op0=ALU.add, op1=ALU.add).then_inc(pj_read, 1)

        @block.tensor
        def _(pe):
            pe.sem_inc(score_read, SCB)
            pe.sem_inc(slot_free, SLOTS)
            pe.sem_inc(o_read, 1)
            pe.wait_ge(const_in, 16 * 8)
            pe.wait_ge(const_set, 6)
            image = qkhl[:, :].rearrange("p (a h w) -> p a h w", a=2, w=HW)

            def fill_aux(j, b, kind, f, n):
                bank = aux[:, n % AXB, :]
                if kind in ("relw", "relh"):
                    for i in range(8):
                        at = 8 * f + i
                        d, query = (1, image[:, at // HW, :, at % HW]) if kind == "relw" else (0, image[:, :, at, :])
                        to = bank[0:SIDE, SIDE * i:SIDE * (i + 1)]
                        mm = pe.matmul(to if d else to.rearrange("p (a w) -> p a w", a=2),
                                       tab[:, d, SIDE - 1 - at:2 * SIDE - 1 - at], query, start=True, stop=True)
                    mm.then_inc(rel_filled, 1)
                elif kind == "max":
                    t, m = divmod(f, MAXB)
                    if f == 0:
                        pe.wait_ge(key_in, 32 * (j + 1))
                    if t % QG == 0 and m == 0:
                        pe.wait_ge(first_hi, j * GRP + t // QG + 1)
                    w = min(512, N - 512 * m)
                    pe.matmul(bank[:, 0:w], hi[:, b, t * P:(t + 1) * P], mkeys[:, 512 * m:512 * m + w],
                              start=True, stop=True).then_inc(max_filled, 1)
                else:
                    pe.wait_ge(diag_ready, j * GRP + f + 1)
                    pe.matmul(bank[:, 0:BLK], rowsel[:, :], diag[:, f % 2, :, :].rearrange("p t q -> p (t q)"),
                              start=True, stop=True).then_inc(bias_filled, 1)

            def read(j, kind, f, n):
                if kind in ("relw", "relh"):
                    pe.wait_ge(rel_read, j * REL + REL_ORDER.index((kind, f)) + 1)
                elif kind == "max":
                    pe.wait_ge(max_read, j * MAXF + f + 1)
                else:
                    pe.wait_ge(bias_read, j * GRP + f + 1)

            order = [x_ for fills in plan for x_ in fills if x_[0] != "norm"]

            def norm_fill(u, f):
                if f == 0:
                    pe.wait_ge(o_read, u * QB + 1)
                pe.matmul(aux[:, f, 0:QUART], densel[:, :], oraw[:, f, :], start=True, stop=True)\
                  .then_inc(norm_filled, 1)

            def attend(u, b, e):
                qb, c = divmod(e, CPH)
                if e == 0:
                    pe.wait_ge(vu_ready, u + 1)
                if c == 0:
                    pe.wait_ge(o_read, u * QB + qb + 1)
                pe.wait_ge(score_read, u * NSB + 4 * (e + 1) + SCB)
                for a_ in range(2):
                    for j in range(4):
                        mm = pe.matmul(out_ps[32 * j:32 * j + 32, 0:QUART], vu[:, b, a_ * CPH + c, :],
                                       probs[:, (2 * (PAIRS * b + e) + a_) % (2 * SLOTS), j * QUART:(j + 1) * QUART],
                                       start=(c == 0 and a_ == 0), stop=(c == CPH - 1 and a_ == 1))
                mm.then_inc(slot_free, 1)

            def aux_fills(u, b, items, n, prev, nxt):
                for kind, f in items:
                    if kind == "norm":
                        if prev and nxt:
                            read(u + 1, *order[n - AXB + f], n - AXB + f)
                        elif prev:
                            read(u, *order[f - AXB], len(order) + f - AXB)
                        if prev:
                            norm_fill(u, f)
                        continue
                    if not nxt:
                        continue
                    if prev and NORM_AT <= n < NORM_AT + QB:
                        pe.wait_ge(norm_read, QB * (u - 1) + n - NORM_AT + 1)
                    elif n >= AXB:
                        read(u + 1, *order[n - AXB], n - AXB)
                    elif prev is not None:
                        read(u, *order[n - AXB], len(order) + n - AXB)
                    fill_aux(u + 1, 1 - b, kind, f, n)
                    n += 1
                return n

            def first(u, v, layer):
                pe.wait_ge(split, u + 1)
                n = 0
                for items in plan:
                    n = aux_fills(u - 1, 1, items, n, None, True)

            def phase(u, v, h, b, prev, nxt, nxt2):
                n = 0
                for k in range(NSB):
                    e, a_ = k // 4, k // 2 % 2
                    qb, c = divmod(e, CPH)
                    par, place = (QB * b + qb) % 2, c % RING
                    turn = v * QB + (QB * b + qb) // 2
                    if k == 0:
                        pe.wait_ge(skey_in, u * 64 + 64)
                    if k % (4 * CPH) == 0:
                        pe.wait_ge(common_in[par], turn * 128 + 128)
                    if k % 4 == 0:
                        pe.wait_ge(row_in[par][place], turn * 32 * (CPH // RING) + 32 * (c // RING + 1))
                    pe.wait_ge(score_read, u * NSB + k + 1)
                    key = a_ * (N // 2) + c * P
                    pe.matmul(score[:, k % SCB, 0:BLK], keys[:, b, key:key + P],
                              moving[:, par, place, a_, k % 2 * BLK:(k % 2 + 1) * BLK],
                              start=True, stop=True).then_inc(score_filled, 1)
                    if k == 0 and nxt:
                        pe.wait_ge(split, u + 2)
                    n = aux_fills(u, b, plan[k], n, prev, nxt)
                    if k % 4 == 2:
                        if e:
                            attend(u, b, e - 1)
                        elif prev:
                            attend(u - 1, 1 - b, PAIRS - 1)

            def last(u):
                attend(u - 1, 1, PAIRS - 1)
                for f in range(QB):
                    pe.wait_ge(norm_read, QB * (u - 1))
                    norm_fill(u, f)

            with pe.Fori(0, LAYERS) as layer:
                pe.wait_ge(gn_ready, layer * 3 + 1)
                pe.matmul(aux[0:HALF, 0, 0:4], gmat[:, :], mv[:, :, 0], start=True, stop=True).then_inc(gn_sum, 1)
                pe.wait_ge(gn_ready, layer * 3 + 2)
                pe.matmul(aux[0:HALF, 0, 0:4], gmat[:, :], gv[:, :], start=True, stop=True).then_inc(gn_sum, 1)
                for f in range(QKF):
                    k, s = divmod(f, PF)
                    b, m = divmod(k, 3)
                    if m == 0 and s == 0:
                        pe.wait_ge(xn_ready, layer * 4 + 2 * b + 2)
                    if f >= 2:
                        pe.wait_ge(qk_read, layer * (QKF + VF) + f - 1)
                    for a_ in range(2):
                        q = b * N + s * SBW + a_ * BLK
                        for t in range(2):
                            mm = pe.matmul(proj[:, f % 2, a_, 0:BLK], wqkv[:, t, m * P:(m + 1) * P], xn[:, t, q:q + BLK],
                                           start=(t == 0), stop=(t == 1))
                    mm.then_inc(qk_filled, 1)
                for v in range(VF):
                    f = QKF + v
                    pe.wait_ge(qk_read, layer * (QKF + VF) + f - 1)
                    for i in range(4):
                        to = proj[:, f % 2, i // 2, (i % 2) * CH:(i % 2 + 1) * CH]
                        tok = (4 * v + i) * P
                        pe.matmul(to, ones[:, :], bv[:, :], start=True, stop=False)
                        for t in range(2):
                            mm = pe.matmul(to, xn[:, t, tok:tok + P], wqkv[:, t, 2 * CH:3 * CH],
                                           start=False, stop=(t == 1))
                    mm.then_inc(qk_filled, 1)
                pe.wait_ge(qk_read, (layer + 1) * (QKF + VF))
                run_units(pe, layer, first, phase, last)
                pe.wait_ge(o_loaded, 32 * (layer + 1))
                for f in range(PJF):
                    i, blk = divmod(f, PF)
                    b, m = divmod(i, 2)
                    if f >= 2:
                        pe.wait_ge(pj_read, layer * PJF + f - 1)
                    else:
                        pe.wait_ge(score_read, (layer + 1) * UNITS * NSB + SCB)
                    for a_ in range(2):
                        q = b * N + blk * SBW + a_ * BLK
                        for t in range(2):
                            mm = pe.matmul(proj[0:HALF, f % 2, a_, 0:BLK], wproj[:, t, m * HALF:(m + 1) * HALF],
                                           xn[:, t, q:q + BLK], start=(t == 0), stop=(t == 1))
                    mm.then_inc(pj_filled, 1)


def kernel(**inputs):
    import numpy as np
    import concourse.bacc as bacc
    from concourse.bass_utils import run_bass_kernel_spmd

    names = [("L0_conv_", "qkv_w", "proj_w", "proj_b"), ("L1_conv_", "qkv_w", "proj_w", "proj_b"),
             ("L2_conv_", "qkv_w", "proj_w", "proj_b"), ("L3_conv_", "Wqkv", "Wproj", "bproj")]
    get = lambda n: np.asarray(inputs[n])
    wqkv = np.stack([get(p + q) for p, q, _, _ in names])
    wproj = np.stack([get(p + w) for p, _, w, _ in names])
    bproj = np.stack([get(p + v).reshape(2, HALF).T for p, _, _, v in names])
    bqkv = np.stack([get(p + "qkv_b") if p + "qkv_b" in inputs else np.zeros(3 * CH, np.float32)
                     for p, _, _, _ in names])
    rel = np.zeros((LAYERS, P, 2, TBW), np.float32)
    for layer, (p, _, _, _) in enumerate(names):
        for d, name in enumerate(("rel_pos_h", "rel_pos_w")):
            r = get(p + name)
            take = np.minimum(np.arange(2 * SIDE - 2, -1, -1), r.shape[0] - 1)
            for part in (0, 16, 64, 80):
                rel[layer, part:part + DH, d, 0:2 * SIDE - 1] = r[take].T
    key = np.arange(N)
    krow, kcol = key % (N // 2) // HW, key // (N // 2) * HW + key % HW
    max_onehot = np.zeros((P, N), np.float32)
    max_onehot[krow, key] = 1.0
    max_onehot[64 + kcol, key] = 1.0
    key_onehot = np.zeros((P, N), np.float32)
    first_row = key % (N // 2) // P * P // HW
    for p in (0, ROWS):
        key_onehot[p + krow - first_row, key] = 1.0
    for p in (16, 16 + HW):
        key_onehot[p + key % HW, key] = 1.0
    rowsel = np.zeros((P, P), np.float32)
    rowsel[:, 0:SIDE] = 1.0
    densel = np.zeros((P, P), np.float32)
    for j in range(4):
        densel[32 * j + DH, 32 * j:32 * j + 32] = 1.0
    per = CH // GROUPS
    ch = np.arange(HALF) // per
    gmat = (ch[:, None] == ch[None, :]).astype(np.float32) / np.float32(per)
    part = np.arange(P) % 64
    hlmask = np.stack([part < 16, (part >= 16) & (part < 32)], axis=1).astype(np.float32)
    chan = np.arange(3 * P).reshape(3, P).T
    qkscale = np.where(chan < CH, 1.0, float(DH) ** -0.5).astype(np.float32)
    arrays = {
        "x": get("x").reshape(IMAGES, SIDE, 2, HW, CH).transpose(4, 0, 2, 1, 3).reshape(CH, TOK), "wqkv0": wqkv[:, 0:HALF], "wqkv1": wqkv[:, HALF:],
        "wproj0": wproj[:, 0:HALF], "wproj1": wproj[:, HALF:], "bproj": bproj,
        "bqk": bqkv[:, 0:2 * CH].reshape(LAYERS, 3, P).transpose(0, 2, 1), "bv": bqkv[:, None, 2 * CH:],
        "rel": rel, "max_onehot": max_onehot, "key_onehot": key_onehot, "ident": np.eye(P, dtype=np.float32), "rowsel": rowsel,
        "densel": densel, "gmat": gmat, "hlmask": hlmask, "qkscale": qkscale,
    }
    arrays = {n: np.ascontiguousarray(v) for n, v in arrays.items()}
    nc = bacc.Bacc("TRN2", target_bir_lowering=False, num_devices=1)
    a = {n: nc.dram_tensor(f"in_{n}", v.shape, mybir.dt.from_np(v.dtype), kind="ExternalInput").ap()
         for n, v in arrays.items()}
    a["out"] = nc.dram_tensor("out_x", (CH, TOK), F32, kind="ExternalOutput").ap()
    build(nc, a)
    r = run_bass_kernel_spmd(nc, [{f"in_{n}": v for n, v in arrays.items()}], core_ids=[0])
    out = r.results[0]["out_x"]
    out = out.reshape(CH, IMAGES, 2, SIDE, HW).transpose(1, 3, 2, 4, 0)
    return np.ascontiguousarray(out).reshape(IMAGES, SIDE, SIDE, CH)
```

```python
from contextlib import ExitStack

import concourse.bass as bass
from concourse import mybir

F32 = mybir.dt.float32
F32R = mybir.dt.float32r
ACT = mybir.ActivationFunctionType
ALU = mybir.AluOpType
AX = mybir.AxisListType

LAYERS, IMAGES, SIDE, CH, HEADS = 4, 2, 48, 192, 12
GROUPS, EPS = 32, 1e-5
DH = CH // HEADS
N = SIDE * SIDE
TOK = IMAGES * N
HALF = CH // 2
UNITS = IMAGES * HEADS
P = 128
KT = N // P
HW = SIDE // 2
CPH = N // 2 // P
ROWS = 6
BLK = 384
GRP = N // BLK
QG = BLK // P
SBW = 2 * BLK
QB = N // SBW
PAIRS = QB * CPH
SCB = 3
AXB = 4
NSB = 4 * PAIRS
SLOTS = 6
QUART = SBW // 4
TBW = 2 * SIDE
MAXB = 5
REL = 2 * GRP
MAXF = KT * MAXB
PF = N // SBW
QKF = IMAGES * 3 * PF
VF = TOK // P // 4
PJF = 2 * TOK // SBW
SPLIT_AT = 72
COMMON = 8
KEY_LOAD = {1: (0, 1), 2: (2,), 3: (3,)}
REP_LOAD = {4: (0,), 5: (1,), 6: (2,), 9: (3, 4, 5), 10: (6, 7)}
OUT_AT = 11
SUMS_AT = 3
RING = 3
REL_ORDER = [("relw", 0), ("relw", 1), ("relw", 2)] + [("relh", r) for r in range(GRP)] \
    + [("relw", 3), ("relw", 4), ("relw", 5)]
REL_FIRST = 6
REL_BEHIND = {3: 6, 6: 7, 9: 8, 13: 9, 17: 10, 21: 11}
NORM_AT = (6, 7, 8)
INVERT_AT = (12, 20, 28)
TAIL = 3
FIRST_HIGH = {("relh", 1): 0, ("relh", 3): 1, ("relh", 5): 2, ("max", 26): 3, ("max", 32): 4, ("max", 38): 5}
V_FIRST = 7
BESIDE = {3 + 2 * i: ("v", V_FIRST + i) for i in range(VF - V_FIRST)}
BESIDE.update({8 + 6 * i: ("qk", QKF // 2 + i) for i in range(QKF // 2)})
GN_LINKS = 14


def schedule():
    seq = []
    for g in range(GRP):
        for k in range(QG * MAXB):
            f = g * QG * MAXB + k
            seq.append([("max", f)])
            if f in REL_BEHIND:
                seq.append([REL_ORDER[REL_BEHIND[f]]])
            if g and k == 9:
                seq.append([("bias", g - 1)])
    seq = [[r] for r in REL_ORDER[:REL_FIRST]] + seq
    for f in reversed(range(QB)):
        seq.insert(NORM_AT[f], [("norm", f)])
    head = seq[:NORM_AT[-1] + QB]
    rest = [i[0] for i in seq[len(head):]]
    places = NSB - len(head) - TAIL
    cuts = [-(-len(rest) * k // places) for k in range(places + 1)]
    return head + [rest[cuts[k]:cuts[k + 1]] for k in range(places)] + [[]] * (TAIL - 1) + [[("bias", GRP - 1)]]


def build(nc, a):
    plan = schedule()
    with ExitStack() as ctx:
        def sb(name, shape, dt=F32):
            return ctx.enter_context(nc.sbuf_tensor(name, shape, dt))

        def ps(name, shape):
            return ctx.enter_context(nc.psum_tensor(name, shape, F32))

        def sem(name):
            return ctx.enter_context(nc.semaphore(name))

        qk_dram = nc.dram_tensor("qk_scratch", (2 * CH, TOK), F32).ap()
        ao_dram = nc.dram_tensor("attention_scratch", (CH, TOK), F32).ap()
        x_dram = nc.dram_tensor("x_scratch", (CH, TOK), F32).ap()

        region = sb("region", [P, 2 * TOK])
        xn = region[0:HALF, :].rearrange("p (t n) -> p t n", t=2)
        probs = region[:, :].rearrange("p (s n) -> p s n", s=2 * SLOTS)
        vall = sb("vall", [P, TOK // P, CH])
        vu = sb("vu", [P, 2, KT, 32])
        full = sb("full", [P, N])
        qkrep = sb("qkrep", [P, N])
        qkhl = sb("qkhl", [P, N], F32R)
        hi = sb("hi", [P, 2, N], F32R)
        lo = sb("lo", [P, 2, N], F32R)
        mkeys = sb("mkeys", [P, N], F32R)
        keys = sb("keys", [P, 2, N], F32R)
        moving = sb("moving", [P, 2, RING, 2, SBW], F32R)
        wproj = sb("wproj", [HALF, 2, CH])
        tab = sb("tab", [P, 2, TBW], F32R)
        ident = sb("ident", [P, P])
        rowsel = sb("rowsel", [P, P], F32R)
        densel = sb("densel", [P, P])
        gmat = sb("gmat", [HALF, HALF])
        hlmask = sb("hlmask", [P, 2])
        qkscale = sb("qkscale", [P, 3])
        bqk = sb("bqk", [P, 3])
        bqks = sb("bqks", [P, 3])
        bproj = sb("bproj", [HALF, 2])
        mpart = sb("mpart", [P, 2, QG, MAXB])
        mcol = sb("mcol", [P, 2, QG])
        diag = sb("diag", [P, 2, QG, P], F32R)
        oraw = sb("oraw", [P, QB, QUART])
        orec = sb("orec", [P, QB, QUART])
        start = lo[:, 1, :].bitcast(F32)
        wqkv = start[0:HALF, 0:6 * CH].rearrange("p (t c) -> p t c", t=2)
        bv = start[:, 6 * CH:7 * CH]
        tabf, tabh = (start[:, 7 * CH + i * 2 * TBW:7 * CH + (i + 1) * 2 * TBW].rearrange("p (d k) -> p d k", d=2)
                      for i in range(2))
        stats = start[0:HALF, 7 * CH + 4 * TBW:7 * CH + 4 * TBW + 4 * GRP * 6]\
            .rearrange("p (i s k) -> p i s k", i=4, k=6)
        mv = sb("mv", [HALF, 4, 2])
        gm = sb("gm", [HALF, 4])
        gt = sb("gt", [HALF, 4])
        gv = sb("gv", [HALF, 4])
        gs = sb("gs", [HALF, 4])
        gr = sb("gr", [HALF, 4])
        gn = sb("gn", [HALF, 4])

        work = ps("work", [P, 1 + SCB + AXB, 512])
        sums = work[:, 0, :]
        score = work[:, 1:1 + SCB, :]
        aux = work[:, 1 + SCB:1 + SCB + AXB, :]
        proj = work[:, 0:4, :].rearrange("p (f a) q -> p f a q", a=2)

        const_in = sem("const_in")
        x_copied = sem("x_copied")
        x_in = sem("x_in")
        piece_in = [sem("piece_in_full"), sem("piece_in_rep")]
        piece_out = [sem("piece_out_full"), sem("piece_out_rep")]
        weights_in = sem("weights_in")
        const_set = sem("const_set")
        pool_set = sem("pool_set")
        gn_link = sem("gn_link")
        gn_sum = sem("gn_sum")
        gn_ready = sem("gn_ready")
        gn_root = sem("gn_root")
        xn_ready = sem("xn_ready")
        qk_filled = sem("qk_filled")
        qk_read = sem("qk_read")
        v_filled = sem("v_filled")
        v_read = sem("v_read")
        qk_stored = [[sem(f"qk_stored_{b}{s}") for s in range(PF)] for b in range(IMAGES)]
        rep_in = sem("rep_in")
        full_in = [sem("full_in_0"), sem("full_in_1")]
        split_high = sem("split_high")
        split = sem("split")
        key_in = sem("key_in")
        skey_in = sem("skey_in")
        common_in = [sem("common_in_0"), sem("common_in_1")]
        row_in = [[sem(f"row_in_{p}{s}") for s in range(RING)] for p in range(2)]
        vu_ready = sem("vu_ready")
        rel_filled = sem("rel_filled")
        rel_read = sem("rel_read")
        first_hi = sem("first_hi")
        max_filled = sem("max_filled")
        max_read = sem("max_read")
        top_ready = sem("top_ready")
        diag_ready = sem("diag_ready")
        bias_filled = sem("bias_filled")
        bias_read = sem("bias_read")
        hi_ready = sem("hi_ready")
        lo_ready = sem("lo_ready")
        score_filled = sem("score_filled")
        score_read = sem("score_read")
        slot_free = sem("slot_free")
        o_read = sem("o_read")
        norm_filled = sem("norm_filled")
        norm_read = sem("norm_read")
        inverse_ready = sem("inverse_ready")
        o_ready = sem("o_ready")
        o_stored = sem("o_stored")
        o_loaded = [sem("o_loaded_0"), sem("o_loaded_1")]
        pj_filled = sem("pj_filled")
        pj_read = sem("pj_read")
        stored = sem("stored")

        def run_units(eng, layer, first, phase, last):
            base = layer * UNITS
            pair = layer * HEADS
            first(eng.snap(base), eng.snap(pair), layer)
            phase(eng.snap(base), eng.snap(pair), 0, 0, False, True, True)
            with eng.Fori(0, HEADS - 2) as h:
                phase(eng.snap(base + h * 2 + 1), eng.snap(pair + h), h, 1, True, True, True)
                phase(eng.snap(base + h * 2 + 2), eng.snap(pair + h + 1), h + 1, 0, True, True, True)
            phase(eng.snap(base + UNITS - 3), eng.snap(pair + HEADS - 2), HEADS - 2, 1, True, True, True)
            phase(eng.snap(base + UNITS - 2), eng.snap(pair + HEADS - 1), HEADS - 1, 0, True, True, False)
            phase(eng.snap(base + UNITS - 1), eng.snap(pair + HEADS - 1), HEADS - 1, 1, True, False, False)
            last(eng.snap(base + UNITS))

        block = ctx.enter_context(nc.Block())

        @block.sync
        def _(sp):
            for dst, name in ((full[:, :], "max_onehot"), (qkrep[:, :], "key_onehot"), (region[:, 0:P], "rowsel"),
                              (ident[:, :], "ident"), (densel[:, :], "densel"), (gmat[:, :], "gmat"),
                              (hlmask[:, :], "hlmask"), (qkscale[:, :], "qkscale")):
                sp.dma_start(dst, a[name]).then_inc(const_in, 16)
            sp.dma_start(x_dram, a["x"]).then_inc(x_copied, 16)
            sp.wait_ge(x_copied, 16)

            def settle():
                sp.wait_ge(const_set, 5)

            def rep_load(h, b, i):
                k = i // 2 % 2
                sp.dma_start(qkrep[i * DH:(i + 1) * DH, :],
                             qk_dram[bass.ds(h * DH + k * CH, DH), b * N:(b + 1) * N]).then_inc(rep_in, 16)

            def full_load(h, b, half):
                for p in (48, 112):
                    sp.dma_start(full[p:p + DH, half * N // 2:(half + 1) * N // 2],
                                 qk_dram[bass.ds(h * DH, DH), b * N + half * N // 2:b * N + (half + 1) * N // 2])\
                      .then_inc(full_in[half], 16)

            def max_key_load():
                for p, src in ((48, 32), (112, 96)):
                    sp.dma_start(mkeys[p:p + DH, :].bitcast(F32), qkhl[src:src + DH, :].bitcast(F32))\
                      .then_inc(key_in, 16)

            def key_load(b, r):
                src = (32, 96, 48, 112)[r]
                sp.dma_start(keys[64 + r * DH:64 + (r + 1) * DH, b, :].bitcast(F32),
                             qkhl[src:src + DH, :].bitcast(F32)).then_inc(skey_in, 16)

            def row_load(b, qb, c):
                par, cols, h0 = (QB * b + qb) % 2, slice(qb * SBW, (qb + 1) * SBW), c * P // HW
                for p, part in ((0, hi), (ROWS, lo)):
                    src = part[h0:h0 + ROWS, b, cols].bitcast(F32)
                    sp.dma_start(moving[p:p + ROWS, par, c % RING, :, :].bitcast(F32),
                                 src.unsqueeze(1).broadcast_to((ROWS, 2, SBW))).then_inc(row_in[par][c % RING], 16)

            def common_load(b, qb, i):
                par, cols = (QB * b + qb) % 2, slice(qb * SBW, (qb + 1) * SBW)
                if i < 4:
                    p, src, part = ((64, 48, hi), (80, 112, hi), (96, 48, lo), (112, 112, lo))[i]
                    sp.dma_start(moving[p:p + DH, par, :, :, :].rearrange("p s a q -> p (s a) q").bitcast(F32),
                                 part[src:src + DH, b, cols].bitcast(F32)
                                 .unsqueeze(1).broadcast_to((DH, 2 * RING, SBW)))\
                      .then_inc(common_in[par], 16)
                else:
                    a_ = i % 2
                    p, part = ((16, hi), (16 + HW, lo))[i // 2 - 2]
                    sp.dma_start(moving[p:p + HW, par, :, a_, :].bitcast(F32),
                                 part[64 + a_ * HW:64 + (a_ + 1) * HW, b, cols].bitcast(F32)
                                 .unsqueeze(1).broadcast_to((HW, RING, SBW))).then_inc(common_in[par], 16)

            def qk_store(layer, f):
                b, m, third = f // (QKF // 2), f // PF % 3, f % PF
                cols = slice(third * SBW, (third + 1) * SBW)
                sp.wait_ge(qk_read, layer * QKF + f + 1)
                sp.dma_start(qk_dram[m * P:(m + 1) * P, b * N + third * SBW:b * N + (third + 1) * SBW],
                             (full, qkrep)[b][:, cols]).then_inc(qk_stored[b][third], 16)

            def first(u, v, layer):
                for f in range(QKF // 2):
                    qk_store(layer, f)
                for third in range(PF):
                    sp.wait_ge(qk_stored[0][third], (layer + 1) * 3 * 16)
                for i in range(8):
                    rep_load(0, 0, i)
                for half in range(2):
                    full_load(0, 0, half)
                sp.wait_ge(split, u + 1)
                max_key_load()
                for r in range(4):
                    key_load(0, r)
                for f in range(QKF // 2, QKF):
                    qk_store(layer, f)
                for third in range(PF):
                    sp.wait_ge(qk_stored[1][third], (layer + 1) * 3 * 16)
                for i in range(8):
                    rep_load(0, 1, i)
                sp.wait_ge(lo_ready, u * GRP + 2)
                for i in range(COMMON):
                    common_load(0, 0, i)
                row_load(0, 0, 0)
                sp.wait_ge(split, u + 2)
                row_load(0, 0, 1)

            def out_store(u, h, b, j):
                if j == 0:
                    sp.wait_ge(o_ready, u + 1)
                    settle()
                to = ao_dram[bass.ds(h * DH, DH), b * N:(b + 1) * N].rearrange("p (a j q) -> p a j q", a=QB, j=4)
                sp.dma_start(to[:, :, j, :], orec[32 * j:32 * j + DH, :, :]).then_inc(o_stored, 16)

            def phase(u, v, h, b, prev, nxt, nxt2):
                for e in range(PAIRS):
                    qb, c = divmod(e, CPH)
                    if e == 0:
                        sp.wait_ge(lo_ready, (u + 1) * GRP - 1)
                    elif c == 0 and (nxt or qb + 1 < QB):
                        sp.wait_ge(lo_ready, (u + 1) * GRP if qb + 1 < QB else (u + 1) * GRP + 2)
                    if c == 0:
                        row_load(b, qb, 2)
                    if e == 0 and nxt:
                        full_load(h + b, 1 - b, 0)
                        sp.wait_ge(max_read, (u + 1) * MAXF)
                        max_key_load()
                    if e == 1:
                        sp.wait_ge(score_filled, u * NSB + 1)
                    elif c and (nxt or e < PAIRS - CPH + 1 or 2 <= c < CPH - 1):
                        sp.wait_ge(score_filled, u * NSB + 4 * (e - 1))
                    if 2 <= c < CPH - 1:
                        row_load(b, qb, c + 1)
                    if e == 2 and nxt:
                        sp.wait_ge(lo_ready, (u + 1) * GRP)
                        full_load(h + b, 1 - b, 1)
                    if c >= 1:
                        if qb + 1 < QB:
                            common_load(b, qb + 1, c - 1)
                        elif nxt:
                            common_load(1 - b, 0, c - 1)
                    if c in (1, CPH - 1):
                        if qb + 1 < QB:
                            row_load(b, qb + 1, 0 if c == 1 else 1)
                        elif nxt:
                            row_load(1 - b, 0, 0 if c == 1 else 1)
                    if nxt and e in KEY_LOAD:
                        for r in KEY_LOAD[e]:
                            key_load(1 - b, r)
                    if nxt2 and e in REP_LOAD:
                        for i in REP_LOAD[e]:
                            rep_load(h + 1, b, i)
                    if prev and 0 <= e - OUT_AT < 4:
                        out_store(u, h - 1 + b, 1 - b, e - OUT_AT)

            def out_load(b):
                for t in range(2):
                    sp.dma_start(xn[:, t, b * N:(b + 1) * N], ao_dram[t * HALF:(t + 1) * HALF, b * N:(b + 1) * N])\
                      .then_inc(o_loaded[b], 16)

            def piece(i):
                return x_dram[(i % 2) * HALF:(i % 2 + 1) * HALF, i // 2 * N:(i // 2 + 1) * N]

            def piece_load(i):
                sp.dma_start((full, qkrep)[i % 2][0:HALF, :], piece(i)).then_inc(piece_in[i % 2], 16)

            def last(u):
                sp.wait_ge(slot_free, u * PAIRS + SLOTS)
                piece_load(0)
                sp.wait_ge(o_stored, 64 * (u - 1) + 16)
                out_load(0)
                for j in range(4):
                    out_store(u, HEADS - 1, 1, j)

            with sp.Fori(0, LAYERS) as layer:
                def weight(dst, name):
                    letters = " ".join("abcd"[:len(a[name].shape) - 2])
                    src = a[name][bass.ds(layer, 1)].rearrange(f"o p {letters} -> (o p) {letters}")
                    sp.dma_start(dst, src).then_inc(weights_in, 16)

                sp.wait_ge(const_set, 5)
                for t in (1, 0):
                    sp.wait_ge(piece_out[t], layer * 32 + 16)
                    sp.dma_start(xn[:, t, :], x_dram[t * HALF:(t + 1) * HALF, :]).then_inc(x_in, 16)
                weight(wqkv[:, 0, :], "wqkv0")
                weight(wqkv[:, 1, :], "wqkv1")
                weight(wproj[:, 0, :], "wproj0")
                weight(wproj[:, 1, :], "wproj1")
                weight(bqk[:, :], "bqk")
                weight(bv[:, :], "bv")
                weight(bproj[:, :], "bproj")
                weight(tabf[:, :, :], "rel")
                run_units(sp, layer, first, phase, last)
                sp.wait_ge(o_stored, (layer + 1) * UNITS * 64 + 16)
                out_load(1)

                for i in range(1, 4):
                    if i >= 2:
                        sp.wait_ge(piece_out[i % 2], (layer * 2 + i // 2 + 1) * 16)
                    piece_load(i)
                    sp.wait_ge(pj_read, layer * PJF + PF * i)
                    sp.dma_start(piece(i - 1), (full, qkrep)[(i - 1) % 2][0:HALF, :])\
                      .then_inc(piece_out[(i - 1) % 2], 16)
                sp.wait_ge(pj_read, (layer + 1) * PJF)
                sp.dma_start(piece(3), qkrep[0:HALF, :]).then_inc(piece_out[1], 16)
            for i in range(2):
                sp.wait_ge(piece_out[i], LAYERS * 32 + 16)
            sp.dma_start(a["out"], x_dram).then_inc(stored, 16)
            sp.wait_ge(stored, 16)

        @block.gpsimd
        def _(pool):
            pool.sem_inc(o_ready, 1)
            pool.sem_inc(o_stored, 16)
            for out in piece_out:
                pool.sem_inc(out, 16)
            pool.memset(vu[:, :, :, DH:32], 0.0).then_inc(pool_set, 1)
            pool.wait_ge(pool_set, 1)
            pool.memset(vu[:, :, :, DH:DH + 1], 1.0).then_inc(pool_set, 1)
            pool.wait_ge(pool_set, 2)

            def split_low(j):
                pool.wait_ge(split_high, QB * (j + 1))
                pool.tensor_tensor(qkhl[64:128, :], qkrep[64:128, :], qkhl[64:128, :].bitcast(F32),
                                   ALU.subtract).then_inc(split, 1)

            def values(b, h):
                pool.tensor_copy(vu[:, b, :, 0:DH],
                                 vall[:, b * KT:(b + 1) * KT, bass.ds(h * DH, DH)]).then_inc(vu_ready, 1)

            def prepare(j, h, b, split_next, layer=None):
                values_at = 0 if layer is None else GRP - 1
                for g in range(GRP):
                    cols = slice(g * BLK, (g + 1) * BLK)
                    if g == 0:
                        pool.wait_ge(split, j + 1)
                    if g == 4 and split_next:
                        pool.wait_ge(split, j + 2)
                    if layer is not None and g == values_at:
                        pool.wait_ge(v_read, (layer + 1) * VF)
                    pool.wait_ge(top_ready, j * GRP + g + 1)
                    pool.tensor_tensor(diag[:, g % 2, :, :], ident[:, :].unsqueeze(1).broadcast_to((P, QG, P)),
                                       mcol[:, g % 2, :].unsqueeze(2).broadcast_to((P, QG, P)), ALU.mult)\
                        .then_inc(diag_ready, 1)
                    pool.wait_ge(hi_ready, j * GRP + g + 1)
                    pool.tensor_tensor(lo[:, b, cols], full[:, cols], hi[:, b, cols].bitcast(F32),
                                       ALU.subtract).then_inc(lo_ready, 1)
                    if g == values_at:
                        values(b, h)
                    if g == 3 and split_next:
                        pool.wait_ge(lo_ready, j * GRP + 4)
                        split_low(j + 1)

            def first(u, v, layer):
                split_low(u)
                prepare(u, 0, 0, False, layer)
                pool.wait_ge(vu_ready, u + 1)
                pool.wait_ge(lo_ready, (u + 1) * GRP)
                split_low(u + 1)

            def normalise(u):
                pool.wait_ge(inverse_ready, QB * u)
                pool.tensor_tensor(orec[:, :, :], oraw[:, :, :], orec[:, :, :], ALU.mult).then_inc(o_ready, 1)

            def phase(u, v, h, b, prev, nxt, nxt2):
                if prev:
                    pool.wait_ge(slot_free, u * PAIRS + SLOTS)
                    normalise(u)
                if nxt:
                    prepare(u + 1, h + b, 1 - b, nxt2)

            with pool.Fori(0, LAYERS) as layer:
                run_units(pool, layer, first, phase, normalise)

        @block.scalar
        def _(act):
            def rel_out(j, kind, r, n):
                i = REL_ORDER.index((kind, r))
                act.wait_ge(rel_filled, j * REL + i + 1)
                bank = aux[:, n % AXB, 0:BLK]
                if kind == "relh":
                    to = full[0:SIDE, :].rearrange("p (a h w) -> p a h w", a=2, w=HW)[:, :, 8 * r:8 * r + 8, :]
                    act.activation(to, bank[0:SIDE, :].rearrange("p (h a w) -> p a h w", a=2, w=HW), ACT.Copy)\
                       .then_inc(rel_read, 1)
                else:
                    to = full[64:64 + SIDE, :].rearrange("p (a h w) -> p a h w", a=2, w=HW)
                    to = to[:, r // 3, :, 8 * (r % 3):8 * (r % 3) + 8]
                    act.activation(to, bank[0:SIDE, :].rearrange("p (w h) -> p h w", w=8), ACT.Copy)\
                       .then_inc(rel_read, 1)

            def high(j, b, g, ready):
                cols = slice(g * BLK, (g + 1) * BLK)
                act.activation(hi[:, b, cols], full[:, cols], ACT.Copy).then_inc(ready, 1)

            def high_behind(j, b, kind, f):
                if (kind, f) in FIRST_HIGH:
                    g = FIRST_HIGH[kind, f]
                    before = REL if g >= GRP // 2 else REL_ORDER.index((kind, f)) + 1
                    act.wait_ge(rel_read, j * REL + before)
                    if g in (0, GRP // 2):
                        act.wait_ge(full_in[2 * g // GRP], 32 * (j + 1))
                    high(j, b, g, first_hi)
                elif kind == "bias":
                    act.wait_ge(bias_read, j * GRP + f + 1)
                    high(j, b, f, hi_ready)

            def split_qk(j):
                for part in range(QB):
                    split_part(j, part)

            def split_part(j, part):
                cols = slice(part * SBW, (part + 1) * SBW)
                if part == 0:
                    act.wait_ge(rep_in, 128 * (j + 1))
                act.activation(qkhl[:, cols], qkrep[:, cols], ACT.Copy).then_inc(split_high, 1)

            def qk_out(layer, f):
                b, m, third = f // (QKF // 2), f // PF % 3, f % PF
                if m:
                    act.wait_ge(qk_stored[b][third], (layer * 3 + m) * 16)
                act.wait_ge(qk_filled, layer * QKF + f + 1)
                to = (full, qkrep)[b][:, third * SBW:(third + 1) * SBW].rearrange("p (a q) -> p a q", a=2)
                act.activation(to, proj[:, (f + b * VF) % 2, :, 0:BLK], ACT.Identity, bias=bqks[:, m:m + 1],
                               scale=qkscale[:, m:m + 1]).then_inc(qk_read, 1)

            def first(u, v, layer):
                split_qk(u)
                n = 0
                for k, items in enumerate(plan):
                    if k in BESIDE and BESIDE[k][0] == "qk":
                        if BESIDE[k][1] == QKF // 2:
                            act.wait_ge(split, u + 1)
                        qk_out(layer, BESIDE[k][1])
                    for kind, f in items:
                        if kind in ("relw", "relh"):
                            rel_out(u, kind, f, n)
                        high_behind(u, 0, kind, f)
                        n += kind != "norm"
                act.wait_ge(key_in, 32 * (u + 1))
                act.wait_ge(skey_in, 64 * (u + 1))
                split_qk(u + 1)

            def denominators_out(u, f):
                if f == 0:
                    act.wait_ge(o_stored, 64 * (u - 1) + 16)
                act.wait_ge(norm_filled, QB * (u - 1) + f + 1)
                act.activation(orec[:, f, :], aux[:, f, 0:QUART], ACT.Copy).then_inc(norm_read, 1)

            def last(u):
                for f in range(QB):
                    denominators_out(u, f)

            def phase(u, v, h, b, prev, nxt, nxt2):
                n, late = 0, []
                for k in range(NSB):
                    if k % 4 == 0:
                        act.wait_ge(slot_free, u * PAIRS + k // 4 + 1)
                    act.wait_ge(score_filled, u * NSB + k + 1)
                    act.activation(probs[:, (2 * PAIRS * b + k // 2) % (2 * SLOTS), k % 2 * BLK:(k % 2 + 1) * BLK],
                                   score[:, k % SCB, 0:BLK], ACT.Exp).then_inc(score_read, 1)
                    if prev:
                        for kind, f in plan[k]:
                            if kind == "norm":
                                denominators_out(u, f)
                    if not nxt:
                        continue
                    for f in late:
                        high_behind(u + 1, 1 - b, "bias", f)
                    late = [f for kind, f in plan[k] if kind == "bias"]
                    for kind, r in plan[k]:
                        if kind in ("relw", "relh"):
                            if kind == "relw" and r == 0:
                                act.wait_ge(lo_ready, u * GRP + 3)
                            if kind == "relh" and r == 0:
                                act.wait_ge(lo_ready, (u + 1) * GRP)
                            rel_out(u + 1, kind, r, n)
                        if kind != "bias":
                            high_behind(u + 1, 1 - b, kind, r)
                        n += kind != "norm"
                    if nxt2 and k in (SPLIT_AT + 4, SPLIT_AT + 8):
                        split_part(u + 2, (k - SPLIT_AT) // 4)
                    if k == SPLIT_AT and nxt2:
                        act.wait_ge(key_in, 32 * (u + 2))
                        act.wait_ge(skey_in, 64 * (u + 2))
                        split_part(u + 2, 0)
                if nxt:
                    for f in late:
                        high_behind(u + 1, 1 - b, "bias", f)

            with act.Fori(0, LAYERS) as layer:
                act.wait_ge(gn_ready, layer * 3 + 3)
                act.activation(gs[:, :], gv[:, :], ACT.Sqrt).then_inc(gn_root, 1)
                for f in range(QKF // 2):
                    qk_out(layer, f)
                run_units(act, layer, first, phase, last)

        @block.vector
        def _(dve):
            dve.memset(moving[0:32, :, :, :, :].bitcast(F32), 0.0).then_inc(const_set, 1)
            dve.wait_ge(const_in, 16 * 8)
            dve.tensor_copy(mkeys[:, :], full[:, :]).then_inc(const_set, 1)
            for b in range(IMAGES):
                dve.tensor_copy(keys[:, b, :], qkrep[:, :]).then_inc(const_set, 1)
            dve.tensor_copy(rowsel[:, :], region[:, 0:P]).then_inc(const_set, 1)
            dve.wait_ge(const_set, 5)

            def key_max(j, f, bank):
                t, m = divmod(f, MAXB)
                g = t // QG
                w = min(512, N - 512 * m)
                dve.wait_ge(max_filled, j * MAXF + f + 1)
                dve.tensor_reduce(mpart[:, g % 2, t % QG, m:m + 1], aux[:, bank, 0:w], AX.X, ALU.max)\
                   .then_inc(max_read, 1)
                if f % (QG * MAXB) == QG * MAXB - 1:
                    dve.wait_ge(max_read, j * MAXF + f + 1)
                    dve.tensor_reduce(mcol[:, g % 2, :], mpart[:, g % 2, :, :], AX.X, ALU.max).then_inc(top_ready, 1)

            def subtract_max(j, g, bank):
                cols = slice(g * BLK, (g + 1) * BLK)
                dve.wait_ge(bias_filled, j * GRP + g + 1)
                dve.tensor_tensor(full[:, cols], full[:, cols], aux[:, bank, 0:BLK], ALU.subtract)\
                   .then_inc(bias_read, 1)

            def sums_out(u, b, qb):
                dve.wait_ge(slot_free, u * PAIRS + (qb + 1) * CPH + SLOTS)
                if qb == 0:
                    dve.wait_ge(o_ready, u + 1)
                dve.tensor_copy(oraw[:, qb, :], sums[:, 0:QUART]).then_inc(o_read, 1)

            def values_out(layer, v):
                dve.wait_ge(v_filled, layer * VF + v + 1)
                dve.tensor_tensor(vall[:, 4 * v:4 * v + 4, :].rearrange("p (a t) c -> p a t c", a=2),
                                  proj[:, (QKF // 2 + v) % 2, :, 0:BLK].rearrange("p a (t c) -> p a t c", t=2),
                                  bv.unsqueeze(1).unsqueeze(1).broadcast_to((P, 2, 2, CH)), ALU.add)\
                   .then_inc(v_read, 1)

            def reciprocal(u, f):
                dve.wait_ge(norm_read, QB * (u - 1) + f + 1)
                dve.reciprocal(orec[:, f, :], orec[:, f, :]).then_inc(inverse_ready, 1)

            def fills(u, prev, nxt, layer=None):
                n = 0
                for k, items in enumerate(plan):
                    if prev is None and k in BESIDE and BESIDE[k][0] == "v":
                        values_out(layer, BESIDE[k][1])
                    if prev is not None and k in (4 * CPH + SUMS_AT, 8 * CPH + SUMS_AT):
                        sums_out(u, 1 if prev == 2 else 0, k // (4 * CPH) - 1)
                    if prev and k == SUMS_AT:
                        sums_out(u - 1, 0 if prev == 2 else 1, QB - 1)
                    if prev and k in INVERT_AT:
                        reciprocal(u, INVERT_AT.index(k))
                    for kind, f in items:
                        if kind == "norm":
                            continue
                        if nxt and kind == "max":
                            key_max(u + 1, f, n % AXB)
                        if nxt and kind == "bias":
                            subtract_max(u + 1, f, n % AXB)
                        n += 1

            def first(u, v, layer):
                for v_ in range(V_FIRST):
                    values_out(layer, v_)
                fills(u - 1, None, True, layer)

            def phase(u, v, h, b, prev, nxt, nxt2):
                fills(u, prev and 1 + b, nxt)

            def last(u):
                sums_out(u - 1, 1, QB - 1)
                for f in range(QB):
                    reciprocal(u, f)

            with dve.Fori(0, LAYERS) as layer:
                links = [0]

                def link(ins):
                    links[0] += 1
                    ins.then_inc(gn_link, 1)
                    dve.wait_ge(gn_link, layer * GN_LINKS + links[0])

                dve.wait_ge(x_in, (layer + 1) * 32)
                for t in range(2):
                    for b in range(IMAGES):
                        for s in range(GRP):
                            i = dve.bn_stats(stats[:, 2 * t + b, s, :],
                                             xn[:, t, b * N + s * BLK:b * N + (s + 1) * BLK])
                dve.wait_ge(weights_in, (layer + 1) * 8 * 16)
                link(i)
                dve.tensor_tensor(bqks[:, :], bqk[:, :], qkscale[:, :], ALU.mult)
                for i in range(4):
                    last_ = dve.bn_aggr(mv[:, i, :], stats[:, i, :, :])
                last_.then_inc(gn_ready, 1)
                dve.wait_ge(gn_ready, layer * 3 + 1)
                dve.wait_ge(gn_sum, layer * 2 + 1)
                link(dve.tensor_copy(gm[:, :], aux[0:HALF, 0, 0:4]))
                link(dve.tensor_tensor(gt[:, :], mv[:, :, 0], gm[:, :], ALU.subtract))
                link(dve.tensor_tensor(gt[:, :], gt[:, :], gt[:, :], ALU.mult))
                dve.tensor_tensor(gv[:, :], gt[:, :], mv[:, :, 1], ALU.add).then_inc(gn_ready, 1)
                dve.wait_ge(gn_sum, layer * 2 + 2)
                dve.tensor_scalar(gv[:, :], aux[0:HALF, 0, 0:4], EPS, None, ALU.add).then_inc(gn_ready, 1)
                dve.wait_ge(gn_root, layer + 1)
                dve.wait_ge(gn_ready, layer * 3 + 3)
                link(dve.reciprocal(gr[:, :], gs[:, :]))
                link(dve.tensor_tensor(gt[:, :], gr[:, :], gr[:, :], ALU.mult))
                link(dve.tensor_tensor(gt[:, :], gt[:, :], gv[:, :], ALU.mult))
                link(dve.tensor_scalar(gt[:, :], gt[:, :], -0.5, 1.5, ALU.mult, ALU.add))
                link(dve.tensor_tensor(gr[:, :], gr[:, :], gt[:, :], ALU.mult))
                link(dve.scalar_tensor_tensor(out=gn[:, :], in0=gm[:, :], scalar=-1.0, in1=gr[:, :],
                                              op0=ALU.mult, op1=ALU.mult))
                link(dve.tensor_copy(tab[:, :, :], tabf[:, :, :]))
                link(dve.tensor_tensor(tabh[:, :, :], tabf[:, :, :], tab[:, :, :].bitcast(F32), ALU.subtract))
                link(dve.tensor_scalar(tabh[:, :, :], tabh[:, :, :], hlmask[:, 1:2], None, ALU.mult))
                link(dve.scalar_tensor_tensor(out=tab[:, :, :], in0=tab[:, :, :].bitcast(F32),
                                              scalar=hlmask[:, 0:1], in1=tabh[:, :, :],
                                              op0=ALU.mult, op1=ALU.add))
                assert links[0] == GN_LINKS
                for b in range(IMAGES):
                    for t in range(2):
                        i = 2 * t + b
                        dve.tensor_scalar(xn[:, t, b * N:(b + 1) * N], xn[:, t, b * N:(b + 1) * N], gr[:, i:i + 1],
                                          gn[:, i:i + 1], ALU.mult, ALU.add).then_inc(xn_ready, 1)
                run_units(dve, layer, first, phase, last)
                for f in range(PJF):
                    i, blk = divmod(f, PF)
                    xs = (full, qkrep)[i % 2][0:HALF, blk * SBW:(blk + 1) * SBW].rearrange("p (a q) -> p a q", a=2)
                    if blk == 0:
                        dve.wait_ge(piece_in[i % 2], (layer * 2 + i // 2 + 1) * 16)
                    dve.wait_ge(pj_filled, layer * PJF + f + 1)
                    dve.scalar_tensor_tensor(out=xs, in0=proj[0:HALF, f % 2, :, 0:BLK],
                                             scalar=bproj[:, i % 2:i % 2 + 1], in1=xs, op0=ALU.add, op1=ALU.add).then_inc(pj_read, 1)

        @block.tensor
        def _(pe):
            pe.sem_inc(score_read, SCB)
            pe.sem_inc(slot_free, SLOTS)
            pe.sem_inc(o_read, 1)
            pe.wait_ge(const_in, 16 * 8)
            pe.wait_ge(const_set, 5)
            image = qkhl[:, :].rearrange("p (a h w) -> p a h w", a=2, w=HW)

            def fill_aux(j, b, kind, f, n):
                bank = aux[:, n % AXB, :]
                if kind in ("relw", "relh"):
                    for i in range(8):
                        at = 8 * f + i
                        d, query = (1, image[:, at // HW, :, at % HW]) if kind == "relw" else (0, image[:, :, at, :])
                        to = bank[0:SIDE, SIDE * i:SIDE * (i + 1)]
                        mm = pe.matmul(to if d else to.rearrange("p (a w) -> p a w", a=2),
                                       tab[:, d, SIDE - 1 - at:2 * SIDE - 1 - at], query, start=True, stop=True)
                    mm.then_inc(rel_filled, 1)
                elif kind == "max":
                    t, m = divmod(f, MAXB)
                    if f == 0:
                        pe.wait_ge(key_in, 32 * (j + 1))
                    if t % QG == 0 and m == 0:
                        pe.wait_ge(first_hi, j * GRP + t // QG + 1)
                    w = min(512, N - 512 * m)
                    pe.matmul(bank[:, 0:w], hi[:, b, t * P:(t + 1) * P], mkeys[:, 512 * m:512 * m + w],
                              start=True, stop=True).then_inc(max_filled, 1)
                else:
                    pe.wait_ge(diag_ready, j * GRP + f + 1)
                    pe.matmul(bank[:, 0:BLK], rowsel[:, :], diag[:, f % 2, :, :].rearrange("p t q -> p (t q)"),
                              start=True, stop=True).then_inc(bias_filled, 1)

            def read(j, kind, f, n):
                if kind in ("relw", "relh"):
                    pe.wait_ge(rel_read, j * REL + REL_ORDER.index((kind, f)) + 1)
                elif kind == "max":
                    pe.wait_ge(max_read, j * MAXF + f + 1)
                else:
                    pe.wait_ge(bias_read, j * GRP + f + 1)

            order = [x_ for fills in plan for x_ in fills if x_[0] != "norm"]

            def norm_fill(u, f):
                if f == 0:
                    pe.wait_ge(o_read, u * QB + 1)
                pe.matmul(aux[:, f, 0:QUART], densel[:, :], oraw[:, f, :], start=True, stop=True)\
                  .then_inc(norm_filled, 1)

            def attend(u, b, e):
                qb, c = divmod(e, CPH)
                if e == 0:
                    pe.wait_ge(vu_ready, u + 1)
                if c == 0:
                    pe.wait_ge(o_read, u * QB + qb + 1)
                pe.wait_ge(score_read, u * NSB + 4 * (e + 1) + SCB)
                for a_ in range(2):
                    for j in range(4):
                        mm = pe.matmul(sums[32 * j:32 * j + 32, 0:QUART], vu[:, b, a_ * CPH + c, :],
                                       probs[:, (2 * (PAIRS * b + e) + a_) % (2 * SLOTS), j * QUART:(j + 1) * QUART],
                                       start=(c == 0 and a_ == 0), stop=(c == CPH - 1 and a_ == 1))
                mm.then_inc(slot_free, 1)

            def aux_fills(u, b, items, n, prev, nxt):
                for kind, f in items:
                    if kind == "norm":
                        if prev and nxt:
                            read(u + 1, *order[AXB + f], AXB + f)
                        elif prev:
                            read(u, *order[f - AXB], len(order) + f - AXB)
                        if prev:
                            norm_fill(u, f)
                        continue
                    if not nxt:
                        continue
                    if prev and 2 * AXB <= n < 2 * AXB + QB:
                        pe.wait_ge(norm_read, QB * (u - 1) + n - 2 * AXB + 1)
                    elif n >= AXB:
                        read(u + 1, *order[n - AXB], n - AXB)
                    elif prev is not None:
                        read(u, *order[n - AXB], len(order) + n - AXB)
                    fill_aux(u + 1, 1 - b, kind, f, n)
                    n += 1
                return n

            def qk_fill(layer, f):
                b, m, third = f // (QKF // 2), f // PF % 3, f % PF
                turn = f + b * VF
                if QKF // 2 <= f < QKF // 2 + 2:
                    pe.wait_ge(v_read, layer * VF + VF - 1 + f - QKF // 2)
                elif f >= 2:
                    pe.wait_ge(qk_read, layer * QKF + f - 1)
                for a_ in range(2):
                    q = b * N + third * SBW + a_ * BLK
                    for t in range(2):
                        mm = pe.matmul(proj[:, turn % 2, a_, 0:BLK], wqkv[:, t, m * P:(m + 1) * P], xn[:, t, q:q + BLK],
                                       start=(t == 0), stop=(t == 1))
                mm.then_inc(qk_filled, 1)

            def v_fill(layer, v):
                if v >= 2:
                    pe.wait_ge(v_read, layer * VF + v - 1)
                else:
                    pe.wait_ge(qk_read, layer * QKF + QKF // 2 - 1 + v)
                for i in range(4):
                    to = proj[:, (QKF // 2 + v) % 2, i // 2, (i % 2) * CH:(i % 2 + 1) * CH]
                    tok = (4 * v + i) * P
                    for t in range(2):
                        mm = pe.matmul(to, xn[:, t, tok:tok + P], wqkv[:, t, 2 * CH:3 * CH],
                                       start=(t == 0), stop=(t == 1))
                mm.then_inc(v_filled, 1)

            def first(u, v, layer):
                pe.wait_ge(xn_ready, layer * 4 + 4)
                for v_ in range(V_FIRST):
                    v_fill(layer, v_)
                pe.wait_ge(split, u + 1)
                n = 0
                for k, items in enumerate(plan):
                    if k in BESIDE:
                        kind, f = BESIDE[k]
                        (qk_fill if kind == "qk" else v_fill)(layer, f)
                    n = aux_fills(u - 1, 1, items, n, None, True)
                pe.wait_ge(qk_read, (layer + 1) * QKF)

            def phase(u, v, h, b, prev, nxt, nxt2):
                n = 0
                for k in range(NSB):
                    e, a_ = k // 4, k // 2 % 2
                    qb, c = divmod(e, CPH)
                    par, place = (QB * b + qb) % 2, c % RING
                    turn = v * QB + (QB * b + qb) // 2
                    if k == 0:
                        pe.wait_ge(skey_in, u * 64 + 64)
                    if k % (4 * CPH) == 0:
                        pe.wait_ge(common_in[par], turn * 128 + 128)
                    if k % 4 == 0:
                        pe.wait_ge(row_in[par][place], turn * 32 * (CPH // RING) + 32 * (c // RING + 1))
                    pe.wait_ge(score_read, u * NSB + k + 1)
                    key = a_ * (N // 2) + c * P
                    pe.matmul(score[:, k % SCB, 0:BLK], keys[:, b, key:key + P],
                              moving[:, par, place, a_, k % 2 * BLK:(k % 2 + 1) * BLK],
                              start=True, stop=True).then_inc(score_filled, 1)
                    if k == 0 and nxt:
                        pe.wait_ge(split, u + 2)
                    n = aux_fills(u, b, plan[k], n, prev, nxt)
                    if k % 4 == 2:
                        if e:
                            attend(u, b, e - 1)
                        elif prev:
                            attend(u - 1, 1 - b, PAIRS - 1)

            def last(u):
                attend(u - 1, 1, PAIRS - 1)
                for f in range(QB):
                    pe.wait_ge(norm_read, QB * (u - 1))
                    norm_fill(u, f)

            with pe.Fori(0, LAYERS) as layer:
                pe.wait_ge(gn_ready, layer * 3 + 1)
                pe.matmul(aux[0:HALF, 0, 0:4], gmat[:, :], mv[:, :, 0], start=True, stop=True).then_inc(gn_sum, 1)
                pe.wait_ge(gn_ready, layer * 3 + 2)
                pe.matmul(aux[0:HALF, 0, 0:4], gmat[:, :], gv[:, :], start=True, stop=True).then_inc(gn_sum, 1)
                pe.wait_ge(xn_ready, layer * 4 + 2)
                for f in range(QKF // 2):
                    qk_fill(layer, f)
                run_units(pe, layer, first, phase, last)
                for f in range(PJF):
                    i, blk = divmod(f, PF)
                    b, m = divmod(i, 2)
                    if m == 0 and blk == 0:
                        pe.wait_ge(o_loaded[b], 32 * (layer + 1))
                    if f >= 2:
                        pe.wait_ge(pj_read, layer * PJF + f - 1)
                    else:
                        pe.wait_ge(score_read, (layer + 1) * UNITS * NSB + SCB)
                    for a_ in range(2):
                        q = b * N + blk * SBW + a_ * BLK
                        for t in range(2):
                            mm = pe.matmul(proj[0:HALF, f % 2, a_, 0:BLK], wproj[:, t, m * HALF:(m + 1) * HALF],
                                           xn[:, t, q:q + BLK], start=(t == 0), stop=(t == 1))
                    mm.then_inc(pj_filled, 1)


def kernel(**inputs):
    import numpy as np
    import concourse.bacc as bacc
    from concourse.bass_utils import run_bass_kernel_spmd

    names = [("L0_conv_", "qkv_w", "proj_w", "proj_b"), ("L1_conv_", "qkv_w", "proj_w", "proj_b"),
             ("L2_conv_", "qkv_w", "proj_w", "proj_b"), ("L3_conv_", "Wqkv", "Wproj", "bproj")]
    get = lambda n: np.asarray(inputs[n])
    wqkv = np.stack([get(p + q) for p, q, _, _ in names])
    wproj = np.stack([get(p + w) for p, _, w, _ in names])
    bproj = np.stack([get(p + v).reshape(2, HALF).T for p, _, _, v in names])
    bqkv = np.stack([get(p + "qkv_b") if p + "qkv_b" in inputs else np.zeros(3 * CH, np.float32)
                     for p, _, _, _ in names])
    rel = np.zeros((LAYERS, P, 2, TBW), np.float32)
    for layer, (p, _, _, _) in enumerate(names):
        for d, name in enumerate(("rel_pos_h", "rel_pos_w")):
            r = get(p + name)
            take = np.minimum(np.arange(2 * SIDE - 2, -1, -1), r.shape[0] - 1)
            for part in (0, 16, 64, 80):
                rel[layer, part:part + DH, d, 0:2 * SIDE - 1] = r[take].T
    key = np.arange(N)
    krow, kcol = key % (N // 2) // HW, key // (N // 2) * HW + key % HW
    max_onehot = np.zeros((P, N), np.float32)
    max_onehot[krow, key] = 1.0
    max_onehot[64 + kcol, key] = 1.0
    key_onehot = np.zeros((P, N), np.float32)
    first_row = key % (N // 2) // P * P // HW
    for p in (0, ROWS):
        key_onehot[p + krow - first_row, key] = 1.0
    for p in (16, 16 + HW):
        key_onehot[p + key % HW, key] = 1.0
    rowsel = np.zeros((P, P), np.float32)
    rowsel[:, 0:SIDE] = 1.0
    densel = np.zeros((P, P), np.float32)
    for j in range(4):
        densel[32 * j + DH, 32 * j:32 * j + 32] = 1.0
    per = CH // GROUPS
    ch = np.arange(HALF) // per
    gmat = (ch[:, None] == ch[None, :]).astype(np.float32) / np.float32(per)
    part = np.arange(P) % 64
    hlmask = np.stack([part < 16, (part >= 16) & (part < 32)], axis=1).astype(np.float32)
    chan = np.arange(3 * P).reshape(3, P).T
    qkscale = np.where(chan < CH, 1.0, float(DH) ** -0.5).astype(np.float32)
    arrays = {
        "x": get("x").reshape(IMAGES, SIDE, 2, HW, CH).transpose(4, 0, 2, 1, 3).reshape(CH, TOK),
        "wqkv0": wqkv[:, 0:HALF], "wqkv1": wqkv[:, HALF:], "wproj0": wproj[:, 0:HALF], "wproj1": wproj[:, HALF:],
        "bproj": bproj, "bqk": bqkv[:, 0:2 * CH].reshape(LAYERS, 3, P).transpose(0, 2, 1),
        "bv": np.repeat(bqkv[:, None, 2 * CH:], P, axis=1), "rel": rel, "max_onehot": max_onehot,
        "key_onehot": key_onehot, "ident": np.eye(P, dtype=np.float32), "rowsel": rowsel, "densel": densel,
        "gmat": gmat, "hlmask": hlmask, "qkscale": qkscale,
    }
    arrays = {n: np.ascontiguousarray(v) for n, v in arrays.items()}
    nc = bacc.Bacc("TRN2", target_bir_lowering=False, num_devices=1)
    a = {n: nc.dram_tensor(f"in_{n}", v.shape, mybir.dt.from_np(v.dtype), kind="ExternalInput").ap()
         for n, v in arrays.items()}
    a["out"] = nc.dram_tensor("out_x", (CH, TOK), F32, kind="ExternalOutput").ap()
    build(nc, a)
    r = run_bass_kernel_spmd(nc, [{f"in_{n}": v for n, v in arrays.items()}], core_ids=[0])
    out = r.results[0]["out_x"]
    out = out.reshape(CH, IMAGES, 2, SIDE, HW).transpose(1, 3, 2, 4, 0)
    return np.ascontiguousarray(out).reshape(IMAGES, SIDE, SIDE, CH)
```
